# Optimizing a Trainium2 kernel written in Bass

```python
import numpy as np
import jax
import jax.numpy as jnp

def _softmax(x, axis=-1):
    return jax.nn.softmax(x, axis=axis)

def _gelu(x):
    return jax.nn.gelu(x, approximate=True)

def _silu(x):
    return jax.nn.silu(x)

def _sigmoid(x):
    return jax.nn.sigmoid(x)

def _layernorm(x, axis=-1, eps=1e-05):
    m = jnp.mean(x, axis=axis, keepdims=True)
    v = jnp.var(x, axis=axis, keepdims=True)
    return (x - m) / jnp.sqrt(v + eps)

def _scatter_add(tgt, idx, src, axis=0):
    return tgt.at[idx].add(src)

def _segment_sum(src, seg, n):
    return jax.ops.segment_sum(src, seg, n)
kernel_name = 'mk_adj_resnorm_d1_adj_r2_4fe635'

def setup_inputs(seed: int=0):
    np.random.seed(seed)
    _w = jnp.asarray

    def _rec_inputs():
        import jax
        import jax.numpy as jnp
        _gk = jax.random.key(seed)
        x = 7.22e-05 + 1 * jax.random.normal(jax.random.fold_in(_gk, 1), (32, 256, 256), jnp.float32)
        _a = jax.random.bernoulli(jax.random.fold_in(_gk, 2), 0.0625, (32, 256, 256))
        _a = jnp.logical_or(_a, jnp.swapaxes(_a, -1, -2))
        _a = jnp.logical_or(_a, jnp.eye(256, dtype=bool))
        _af = _a.astype(jnp.float32)
        _af = _af * jax.random.uniform(jax.random.fold_in(_gk, 3), (32, 256, 256), jnp.float32, 0.05, 1)
        adj = _af
        return (x, adj)
    x, adj = _rec_inputs()

    def _L0_gnn_setup():
        import jax, jax.numpy as jnp
        import numpy as np
        EMBED_DIM = 256
        NUM_HEADS = 8
        HEAD_DIM = EMBED_DIM // NUM_HEADS
        SCALE = HEAD_DIM ** (-0.5)
        B, S = (16, 512)
        key = jax.random.key(seed)
        ks = jax.random.split(key, 12)
        init = lambda k, shape: jax.random.normal(k, shape, dtype=jnp.float32) * EMBED_DIM ** (-0.5)
        return {'x': jax.random.normal(ks[0], (B, S, EMBED_DIM), dtype=jnp.float32), 'adj_matrix': jax.random.uniform(ks[1], (B, S, S), dtype=jnp.float32), 'bond_matrix': jax.random.uniform(ks[2], (B, S, S), dtype=jnp.float32), 'Wq': init(ks[3], (EMBED_DIM, EMBED_DIM)), 'bq': jnp.zeros((EMBED_DIM,), jnp.float32), 'Wk': init(ks[4], (EMBED_DIM, EMBED_DIM)), 'bk': jnp.zeros((EMBED_DIM,), jnp.float32), 'Wv': init(ks[5], (EMBED_DIM, EMBED_DIM)), 'bv': jnp.zeros((EMBED_DIM,), jnp.float32), 'Wo': init(ks[6], (EMBED_DIM, EMBED_DIM)), 'bo': jnp.zeros((EMBED_DIM,), jnp.float32), 'seq_len': S}
    _L0_gnn_all = _L0_gnn_setup()
    _L0_gnn_in = {k: v for k, v in _L0_gnn_all.items() if k in ('Wq', 'bq', 'Wk', 'bk', 'Wv', 'bv', 'Wo', 'bo')}
    del _L0_gnn_all
    return {'x': x, 'adj': adj, 'L0_gnn_Wq': _L0_gnn_in['Wq'], 'L0_gnn_bq': _L0_gnn_in['bq'], 'L0_gnn_Wk': _L0_gnn_in['Wk'], 'L0_gnn_bk': _L0_gnn_in['bk'], 'L0_gnn_Wv': _L0_gnn_in['Wv'], 'L0_gnn_bv': _L0_gnn_in['bv'], 'L0_gnn_Wo': _L0_gnn_in['Wo'], 'L0_gnn_bo': _L0_gnn_in['bo']}

def reference(x, adj, L0_gnn_Wq, L0_gnn_bq, L0_gnn_Wk, L0_gnn_bk, L0_gnn_Wv, L0_gnn_bv, L0_gnn_Wo, L0_gnn_bo):
    import jax
    import jax.numpy as jnp

    def _L0_gnn_ref(x, adj_matrix, bond_matrix, Wq, bq, Wk, bk, Wv, bv, Wo, bo, seq_len):
        import jax, jax.numpy as jnp
        import numpy as np
        EMBED_DIM = 256
        NUM_HEADS = 8
        HEAD_DIM = EMBED_DIM // NUM_HEADS
        SCALE = HEAD_DIM ** (-0.5)
        B, S = (16, 512)
        b = x.shape[0]

        def proj(W, bias):
            y = jnp.einsum('bse,fe->bsf', x, W) + bias
            return y.reshape(b, seq_len, NUM_HEADS, HEAD_DIM).transpose(0, 2, 1, 3)
        q, k, v = (proj(Wq, bq), proj(Wk, bk), proj(Wv, bv))
        scores = jnp.einsum('bhqd,bhkd->bhqk', q, k) * SCALE
        mask = (adj_matrix + bond_matrix)[:, None, :, :]
        scores = scores * mask
        attn = jax.nn.softmax(scores, axis=-1)
        ctx = jnp.einsum('bhqk,bhkd->bhqd', attn, v)
        ctx = ctx.transpose(0, 2, 1, 3).reshape(b, seq_len, EMBED_DIM)
        return jnp.einsum('bse,fe->bsf', ctx, Wo) + bo
    x = _layernorm(x + _L0_gnn_ref(x, adj, adj, L0_gnn_Wq, L0_gnn_bq, L0_gnn_Wk, L0_gnn_bk, L0_gnn_Wv, L0_gnn_bv, L0_gnn_Wo, L0_gnn_bo, 256), axis=-1)
    return x

_drawn_inputs = setup_inputs


def setup_inputs(seed=0):
    import zlib

    import numpy as np

    out = dict(_drawn_inputs(seed))
    spreads = {'L0_gnn_bq': (0.0, 0.457),
     'L0_gnn_bk': (0.0, 0.57),
     'L0_gnn_bv': (0.0, 0.1),
     'L0_gnn_bo': (0.0, 0.1)}
    factors = {}
    for name, (base, spread) in spreads.items():
        noise = np.random.default_rng([zlib.crc32(name.encode()), seed]).standard_normal(out[name].shape)
        drawn = base * np.exp(spread * noise) if base else spread * noise
        out[name] = jnp.asarray(drawn.astype(out[name].dtype))
    for name, factor in factors.items():
        out[name] = (out[name] * factor).astype(out[name].dtype)
    return out
```

```python
from contextlib import ExitStack

import concourse.bass as bass
from concourse import mybir
from concourse.alu_op_type import AluOpType as ALU

ACT = mybir.ActivationFunctionType
F32 = mybir.dt.float32
F32R = mybir.dt.float32r

P = 128
B, S, E = 32, 256, 256
H, D = 8, 32
T = S // P
J = P // D
PAIRS = B // 2
LOW = 64
ROWS = LOW + H
EPS = 1e-5
LOWEST = -3.4028234e38
BODY = 4
FIRST = 3
LOOPS = 6

KQ_SLOTS = {1: 0, 2: 1, 4: 2, 5: 3}
V_SLOTS = {1: 0, 5: 1}
COLUMN_BANKS = 3
BANK_AGE = {0: 2, 1: 2, 2: 5}


def build(nc, x, x_t, adj, adj_t, wq, wk, wv, wo, bq, bk, bv, bo, out):
    ctx = ExitStack()
    with ctx:
        def sb(name, shape, dt=F32):
            return ctx.enter_context(nc.sbuf_tensor(name, shape, dt))

        def bank(name):
            return ctx.enter_context(nc.psum_tensor(name, [P, 512], F32))

        def sem(name):
            return ctx.enter_context(nc.semaphore(name))

        xt = sb("xt", [P, 2, T, 2, S])
        xr = sb("xr", [P, 2, 2, T, E])
        adj_rows = sb("adj_rows", [P, 2, 2, T, S])
        adj_cols = sb("adj_cols", [P, 2, 2, T, S])
        w_q, w_k, w_v, w_o = (sb(f"w_{n}", [P, T, E]) for n in "qkvo")
        b_q, b_k, b_v = (sb(f"b_{n}", [P, T]) for n in "qkv")
        b_o = sb("b_o", [1, E])
        bias = sb("bias", [P, E])
        whole = sb("whole", [P, 2, 512])
        parts = sb("parts", [P, 2, 4, T * 512], F32R)
        stack = sb("stack", [P, 2, 2, J, T * 512], F32R)
        v = sb("v", [P, 2, 2, T, E])
        top = sb("top", [P, 2, T, H])
        cut_top = sb("cut_top", [P, 2, T, ROWS], F32R)
        shift = sb("shift", [ROWS, S], F32R)
        pick = sb("pick", [ROWS, H, P], F32R)
        probs = sb("probs", [P, H, T * S])
        folded = sb("folded", [P, H, S])
        inverse = sb("inverse", [P, S])
        context = sb("context", [P, 2, S])
        y = sb("y", [P, T, E])
        stats = sb("stats", [P, T, 6])
        mean_var = sb("mean_var", [P, T, 2])
        scale = sb("scale", [P, 4, T])
        result = sb("result", [P, 2, T, E])
        ident = sb("ident", [P, P])
        ones = sb("ones", [P, P])
        draft = probs[0:ROWS, 0:2, :].rearrange("p a (b k) -> p (a b) k", k=P)

        row_bank = [bank(f"row_bank{n}") for n in range(2)]
        col_bank = [bank(f"col_bank{n}") for n in range(COLUMN_BANKS)]
        ctx_bank = bank("ctx_bank")
        proj_bank = bank("proj_bank")
        out_bank = bank("out_bank")

        weights_in = sem("weights_in")
        xt_in, x_in, adj_in, adj_t_in, stored = (
            [sem(f"{name}{n}") for n in range(2)] for name in ("xt_in", "x_in", "adj_in", "adj_t_in", "stored"))
        stacked = [[sem(f"stacked{n}_{j}") for j in range(J)] for n in range(2)]
        cleared, drafted, constants = sem("cleared"), sem("drafted"), sem("constants")
        picked = sem("picked")
        bias_made, bias_ready = sem("bias_made"), sem("bias_ready")
        kq_made, kq_high, kq_low = sem("kq_made"), sem("kq_high"), sem("kq_low")
        v_made, v_ready = sem("v_made"), sem("v_ready")
        rows_made, rows_used = sem("rows_made"), sem("rows_used")
        top_high, top_cut, top_turned, shift_ready = (
            sem("top_high"), sem("top_cut"), sem("top_turned"), sem("shift_ready"))
        cols_made, masked, shifted, probs_ready = (
            sem("cols_made"), sem("masked"), sem("shifted"), sem("probs_ready"))
        folded_ready = sem("folded_ready")
        ctx_made, inverted, ctx_ready = sem("ctx_made"), sem("inverted"), sem("ctx_ready")
        out_made, y_ready, stats_ready, mean_ready = (
            sem("out_made"), sem("y_ready"), sem("stats_ready"), sem("mean_ready"))
        var_added, sd_inverted, scale_ready = sem("var_added"), sem("sd_inverted"), sem("scale_ready")
        passed_dve, passed_pool = sem("passed_dve"), sem("passed_pool")
        x_ready, result_ready = sem("x_ready"), sem("result_ready")

        def flat(tile):
            return tile.rearrange("p a b c -> p (a b c)")

        out_d = out.rearrange("b (t p) e -> b p t e", p=P)

        def wait(eng, what, value):
            if not isinstance(value, int) or value > 0:
                eng.wait_ge(what, value)

        def head(pair, which, o, b):
            j, t = o // T, o % T
            return stack[:, pair % 2, which, j, t * 512 + b * S:t * 512 + (b + 1) * S]

        def stand_apart(eng, passed):
            eng.sem_inc(passed, 1)

        turn = []

        def run_steps(eng, step):
            for g in range(-3, FIRST):
                step(g, g)
            with eng.Fori(0, LOOPS) as u:
                turn.append(u)
                for k in range(FIRST, FIRST + BODY):
                    step(u * BODY + k, k)
            for g in range(FIRST + LOOPS * BODY, B + 2):
                step(g, g)

        def todo(g, k):
            loop = not isinstance(g, int)
            return {
                "rows": loop or 0 <= g + 1 < B,
                "cols": loop or 0 <= g < B,
                "before": loop or 0 <= g - 1 < B,
                "second": loop or 0 <= g - 2 < B,
                "kq": k % 2 == 1 and (loop or (g + 3) // 2 < PAIRS),
                "v": k % 2 == 0 and (loop or (g + 2) // 2 < PAIRS),
            }

        def half(g, k, add):
            return (g + add) // 2 if isinstance(g, int) else turn[-1] * (BODY // 2) + (k + add) // 2

        def nth(pair, kp):
            return pair // 2 if isinstance(pair, int) else turn[-1] + kp // 2

        block = ctx.enter_context(nc.Block())

        @block.sync
        def _(sp):
            for tile, dram in ((w_k, wk), (w_q, wq), (w_v, wv), (w_o, wo)):
                sp.dma_start(tile[:], dram).then_inc(weights_in, 16)
            for tile, dram in ((b_q, bq), (b_k, bk), (b_v, bv), (b_o, bo)):
                sp.dma_start(tile[:], dram).then_inc(weights_in, 16)
            sp.dma_start(flat(xt[:, 0]), x_t[0]).then_inc(xt_in[0], 16)

            def step(g, k):
                if not todo(g, k)["kq"]:
                    return
                pair, kp = half(g, k, 3), (k + 3) // 2
                if not isinstance(g, int) or g + 5 < 2 * PAIRS:
                    wait(sp, v_made, 2 * pair)
                    sp.dma_start(flat(xt[:, (kp + 1) % 2]), x_t[pair + 1]).then_inc(xt_in[(kp + 1) % 2], 16)
                for which in range(2):
                    wait(sp, kq_low, 4 * pair + 2 * which + 2)
                    for j in range(J):
                        wait(sp, cols_made, 8 * g + 2 * j + 2)
                        for group in range(J):
                            part = group % 2 if which == 0 else group // 2
                            sp.dma_start(stack[D * group:D * (group + 1), kp % 2, which, j, :].bitcast(F32),
                                         parts[D * j:D * (j + 1), kp % 2, 2 * which + part, :].bitcast(F32)
                                         ).then_inc(stacked[kp % 2][j], 16)

            run_steps(sp, step)

        @block.tensor
        def _(pe):
            def rows(n, kn, o):
                if o % T == 0:
                    pe.wait_ge(stacked[(kn // 2) % 2][o // T], nth(half(n, kn, -(kn % 2)), kn // 2) * (8 * 16) + 8 * 16)
                wait(pe, rows_used, 8 * n + o - 1)
                q, key = head(kn // 2, 1, o, kn % 2), head(kn // 2, 0, o, kn % 2)
                for t in range(T):
                    last = nc.tensor.matmul(row_bank[o % 2][:, t * S:(t + 1) * S], q[:, t * P:(t + 1) * P], key,
                                            start=(t == 0), stop=True, skip_group_check=True)
                last.then_inc(rows_made, 1)

            def cols(g, k, o):
                wait(pe, probs_ready, 8 * g + o - BANK_AGE.get(o, COLUMN_BANKS) + 1)
                q, key = head(k // 2, 1, o, k % 2), head(k // 2, 0, o, k % 2)
                for t in range(T):
                    last = nc.tensor.matmul(col_bank[o % COLUMN_BANKS][:, t * S:(t + 1) * S],
                                            key[:, t * P:(t + 1) * P], q,
                                            start=(t == 0), stop=True, skip_group_check=True)
                last.then_inc(cols_made, 1)

            def subtract_top(g, o):
                if o == 0:
                    pe.wait_ge(shift_ready, g + 1)
                pe.wait_ge(masked, 8 * g + o + 1)
                nc.tensor.matmul(col_bank[o % COLUMN_BANKS][:], pick[:, o, :],
                                 shift[:].unsqueeze(1).to_broadcast([ROWS, T, S]),
                                 start=False, stop=True, skip_group_check=True).then_inc(shifted, 1)

            def turn_top(g, k):
                pe.wait_ge(top_cut, g + 1)
                wait(pe, y_ready, g - 1)
                for t in range(T):
                    last = nc.tensor.transpose(out_bank[0:ROWS, t * P:(t + 1) * P],
                                               cut_top[:, k % 2, t, :].bitcast(F32), ident[:])
                last.then_inc(top_turned, 1)

            def project_kq(pair, kp, c):
                w = w_k if c < 2 else w_q
                if c == 0:
                    pe.wait_ge(xt_in[kp % 2], nth(pair, kp) * 16 + 16)
                    wait(pe, v_ready, 2 * pair)
                else:
                    pe.wait_ge(kq_high, 4 * pair + c)
                for t in range(T):
                    last = nc.tensor.matmul(proj_bank[:], w[:, t, (c % 2) * P:(c % 2 + 1) * P],
                                            xt[:, kp % 2, t].rearrange("p b s -> p (b s)"),
                                            start=(t == 0), stop=(t == T - 1))
                last.then_inc(kq_made, 1)

            def project_v(pair, kp, b):
                if b == 0:
                    pe.wait_ge(kq_high, 4 * pair + 4)
                else:
                    pe.wait_ge(v_ready, 2 * pair + 1)
                for n in range(T):
                    for t in range(T):
                        last = nc.tensor.matmul(proj_bank[:, n * E:(n + 1) * E],
                                                xt[:, kp % 2, t, b, n * P:(n + 1) * P], w_v[:, t, :],
                                                start=(n == 0 and t == 0), stop=(t == T - 1),
                                                skip_group_check=True)
                last.then_inc(v_made, 1)

            def weigh_v(g, k, half_):
                if half_ == 0:
                    pe.wait_ge(v_ready, g + 1)
                wait(pe, ctx_ready, 2 * g + half_)
                pe.wait_ge(folded_ready, 4 * g + 2 * half_ + 2)
                heads = range(J * half_, J * half_ + J)
                for t in range(T):
                    for o in heads:
                        c = D * (o % J)
                        nc.tensor.matmul(ctx_bank[c:c + D, 0:S], v[:, (k // 2) % 2, k % 2, t, o * D:(o + 1) * D],
                                         probs[:, o, t * S:(t + 1) * S], start=(t == 0), stop=(t == T - 1),
                                         tile_position=(0, c))
                for o in heads:
                    c = D * (o % J)
                    last = nc.tensor.matmul(ctx_bank[c:c + D, S:2 * S], ones[:, 0:D], folded[:, o, :],
                                            start=True, stop=True, tile_position=(0, c))
                last.then_inc(ctx_made, 1)

            def project_out(g):
                pe.wait_ge(ctx_ready, 2 * g + 2)
                if isinstance(g, int) and g + 1 == B:
                    pe.wait_ge(y_ready, g)
                else:
                    pe.wait_ge(shift_ready, g + 2)
                for n in range(T):
                    for f in range(T):
                        last = nc.tensor.matmul(out_bank[:, n * E:(n + 1) * E], context[:, f, n * P:(n + 1) * P],
                                                w_o[:, f, :], start=(n == 0 and f == 0), stop=(f == T - 1),
                                                skip_group_check=True)
                last.then_inc(out_made, 1)

            pe.wait_ge(constants, 1)
            pe.wait_ge(weights_in, 8 * 16)
            nc.tensor.matmul(out_bank[:, 0:E], ones[0:1, :], b_o[:], start=True, stop=False)
            for f in range(T):
                last = nc.tensor.matmul(out_bank[:, 0:E], b_v[:, f:f + 1].to_broadcast([P, P]), w_o[:, f, :],
                                        start=False, stop=(f == T - 1))
            last.then_inc(bias_made, 1)
            pe.wait_ge(bias_ready, 1)
            pe.wait_ge(picked, 1)

            def step(g, k):
                do = todo(g, k)
                for o in range(H):
                    if do["rows"]:
                        rows(g + 1, k + 1, o)
                    if do["cols"]:
                        cols(g, k, o)
                    if o == 0:
                        if do["before"]:
                            subtract_top(g - 1, H - 1)
                        if do["cols"]:
                            turn_top(g, k)
                    elif do["cols"]:
                        subtract_top(g, o - 1)
                    if do["kq"] and o in KQ_SLOTS:
                        project_kq(half(g, k, 3), (k + 3) // 2, KQ_SLOTS[o])
                    if do["v"] and o in V_SLOTS:
                        project_v(half(g, k, 2), (k + 2) // 2, V_SLOTS[o])
                    if o == 3 and do["before"]:
                        weigh_v(g - 1, k - 1, 1)
                    if o == 6 and do["before"]:
                        project_out(g - 1)
                    if o == 7 and do["cols"]:
                        weigh_v(g, k, 0)

            run_steps(pe, step)

        @block.vector
        def _(dve):
            def reduce_rows(n, kn, o):
                if o == 0:
                    dve.wait_ge(adj_in[(kn // 2) % 2], nth(half(n, kn, -(kn % 2)), kn // 2) * 16 + 16)
                dve.wait_ge(rows_made, 8 * n + o + 1)
                stand_apart(dve, passed_dve)
                for t in range(T):
                    tile = row_bank[o % 2][:, t * S:(t + 1) * S]
                    last = nc.vector.tensor_tensor_reduce(
                        tile, tile, adj_rows[:, (kn // 2) % 2, kn % 2, t, :], 1.0, LOWEST, ALU.mult, ALU.max,
                        top[:, kn % 2, t, o:o + 1])
                last.then_inc(rows_used, 1)

            def cut_tops(n, kn):
                dve.wait_ge(rows_used, 8 * n + 8)
                high, low = cut_top[:, kn % 2, :, 0:H], cut_top[:, kn % 2, :, LOW:ROWS]
                nc.vector.tensor_scalar(high, top[:, kn % 2], -1.0, None, ALU.mult).then_inc(top_high, 1)
                dve.wait_ge(top_high, n + 1)
                nc.vector.scalar_tensor_tensor(low, top[:, kn % 2], -1.0, high.bitcast(F32),
                                               ALU.mult, ALU.subtract).then_inc(top_cut, 1)

            def mask_cols(g, k, o):
                if o == 0:
                    dve.wait_ge(adj_t_in[(k // 2) % 2], nth(half(g, k, -(k % 2)), k // 2) * 16 + 16)
                dve.wait_ge(cols_made, 8 * g + o + 1)
                tile = col_bank[o % COLUMN_BANKS][:]
                nc.vector.tensor_tensor(tile, tile, adj_cols[:, (k // 2) % 2, k % 2].rearrange("p t s -> p (t s)"),
                                        ALU.mult).then_inc(masked, 1)

            def invert(g, half_):
                dve.wait_ge(ctx_made, 2 * g + half_ + 1)
                nc.vector.reciprocal(inverse[:], ctx_bank[:, S:2 * S]).then_inc(inverted, 1)

            def scale_context(g, half_):
                dve.wait_ge(inverted, 2 * g + half_ + 1)
                wait(dve, out_made, g)
                nc.vector.tensor_tensor(context[:, half_, :], ctx_bank[:, 0:S], inverse[:],
                                        ALU.mult).then_inc(ctx_ready, 1)

            def add_residual(g, k):
                dve.wait_ge(out_made, g + 1)
                dve.wait_ge(x_ready, g + 1)
                wait(dve, result_ready, g)
                nc.vector.tensor_tensor(y[:].rearrange("p t e -> p (t e)"), out_bank[:],
                                        xr[:, (k // 2) % 2, k % 2].rearrange("p t e -> p (t e)"),
                                        ALU.add).then_inc(y_ready, 1)

            def row_stats(g):
                dve.wait_ge(y_ready, g + 1)
                for t in range(T):
                    last = nc.vector.bn_stats(stats[:, t, :], y[:, t, :])
                last.then_inc(stats_ready, 1)

            def aggregate(g):
                dve.wait_ge(stats_ready, g + 1)
                wait(dve, scale_ready, g)
                stand_apart(dve, passed_dve)
                for t in range(T):
                    last = nc.vector.bn_aggr(mean_var[:, t, :], stats[:, t, :])
                last.then_inc(mean_ready, 1)

            nc.vector.memset(cut_top[:].bitcast(F32), 0.0)
            nc.vector.memset(scale[:, 1, :], -0.5)
            nc.vector.memset(ones[:], 1.0).then_inc(cleared, 1)
            dve.wait_ge(cleared, 1)
            dve.wait_ge(drafted, 3)
            nc.vector.tensor_copy(pick[:], draft).then_inc(picked, 1)
            dve.wait_ge(bias_made, 1)
            nc.vector.tensor_copy(bias[:], out_bank[:, 0:E]).then_inc(bias_ready, 1)

            def step(g, k):
                do = todo(g, k)
                for o in range(H):
                    if do["rows"]:
                        reduce_rows(g + 1, k + 1, o)
                        if o == H - 1:
                            cut_tops(g + 1, k + 1)
                    if do["cols"]:
                        mask_cols(g, k, o)
                    if do["before"]:
                        if o == 0:
                            invert(g - 1, 0)
                        if o == 1:
                            scale_context(g - 1, 0)
                        if o == 4:
                            invert(g - 1, 1)
                        if o == 5:
                            scale_context(g - 1, 1)
                        if o == 7:
                            add_residual(g - 1, k - 1)
                    if do["second"]:
                        if o == 0:
                            row_stats(g - 2)
                        if o == 1:
                            aggregate(g - 2)

            run_steps(dve, step)

        @block.scalar
        def _(act):
            def load_masks(pair, kp):
                wait(act, masked, 16 * (pair - 1))
                act.dma_start(flat(adj_rows[:, kp % 2]), adj[pair]).then_inc(adj_in[kp % 2], 16)
                act.dma_start(flat(adj_cols[:, kp % 2]), adj_t[pair]).then_inc(adj_t_in[kp % 2], 16)

            def load_x(pair, kp):
                wait(act, y_ready, 2 * (pair - 1))
                act.dma_start(flat(xr[:, kp % 2]), x[pair]).then_inc(x_in[kp % 2], 16)

            def exp(g, k, o):
                act.wait_ge(shifted, 8 * g + o + 1)
                if o % J == 0:
                    wait(act, ctx_made, 2 * g - 1 + o // J)
                nc.scalar.activation(probs[:, o, :], col_bank[o % COLUMN_BANKS][:], ACT.Exp,
                                     scale=2.0 * float(D) ** -0.5).then_inc(probs_ready, 1)

            def copy_shift(g):
                act.wait_ge(top_turned, g + 1)
                nc.scalar.copy(shift[:], out_bank[0:ROWS, 0:S]).then_inc(shift_ready, 1)

            def cut_kq(pair, kp, c):
                act.wait_ge(kq_made, 4 * pair + c + 1)
                wait(act, kq_low, 4 * pair + c - 1)
                b = (b_k if c < 2 else b_q)[:, c % 2:c % 2 + 1]
                nc.scalar.activation(whole[:, c % 2, :], proj_bank[:], ACT.Identity, bias=b)
                nc.scalar.activation(parts[:, kp % 2, 2 * (c // 2), (c % 2) * 512:(c % 2 + 1) * 512],
                                     proj_bank[:], ACT.Identity, bias=b).then_inc(kq_high, 1)

            def copy_v(pair, kp, b):
                act.wait_ge(v_made, 2 * pair + b + 1)
                nc.scalar.copy(v[:, kp % 2, b].rearrange("p t e -> p (t e)"), proj_bank[:]).then_inc(v_ready, 1)

            def normalise(g, k):
                act.wait_ge(scale_ready, g + 1)
                act.wait_ge(stored[k % 2], half(g, k, -(k % 2)) * 16 + 16)
                for t in range(T):
                    last = nc.scalar.activation(result[:, k % 2, t, :], y[:, t, :], ACT.Identity,
                                                bias=scale[:, 3, t:t + 1], scale=scale[:, 2, t:t + 1])
                last.then_inc(result_ready, 1)

            def store(g, k):
                act.wait_ge(result_ready, g + 1)
                act.dma_start(out_d[g], result[:, k % 2]).then_inc(stored[k % 2], 16)

            for n in range(2):
                act.sem_inc(stored[n], 16)
            act.wait_ge(weights_in, 8 * 16)
            act.wait_ge(picked, 1)

            def step(g, k):
                do = todo(g, k)
                for o in range(H):
                    if o == 0:
                        if do["before"]:
                            exp(g - 1, k - 1, H - 1)
                        if do["cols"]:
                            copy_shift(g)
                        if do["v"]:
                            load_masks(half(g, k, 2), (k + 2) // 2)
                        if k % 2 == 1 and do["rows"]:
                            load_x(half(g, k, 1), (k + 1) // 2)
                    elif do["cols"]:
                        exp(g, k, o - 1)
                    if do["kq"] and o in KQ_SLOTS:
                        cut_kq(half(g, k, 3), (k + 3) // 2, KQ_SLOTS[o])
                    if do["v"] and o in V_SLOTS:
                        copy_v(half(g, k, 2), (k + 2) // 2, V_SLOTS[o])
                    if do["second"]:
                        if o == 4:
                            normalise(g - 2, k - 2)
                        if o == 5:
                            store(g - 2, k - 2)

            run_steps(act, step)
            for n in range(2):
                act.wait_ge(stored[n], 16 * (B // 2) + 16)

        @block.gpsimd
        def _(pool):
            def low_kq(pair, kp, c):
                pool.wait_ge(kq_high, 4 * pair + c + 1)
                cut = slice((c % 2) * 512, (c % 2 + 1) * 512)
                nc.gpsimd.tensor_tensor(parts[:, kp % 2, 2 * (c // 2) + 1, cut], whole[:, c % 2, :],
                                        parts[:, kp % 2, 2 * (c // 2), cut].bitcast(F32),
                                        ALU.subtract).then_inc(kq_low, 1)

            def fold(g, i):
                pool.wait_ge(probs_ready, 8 * g + 2 * i + 2)
                wait(pool, ctx_made, 2 * g - 1 + i // 2)
                nc.gpsimd.tensor_tensor(folded[:, 2 * i:2 * i + 2, :], probs[:, 2 * i:2 * i + 2, 0:S],
                                        probs[:, 2 * i:2 * i + 2, S:2 * S], ALU.add).then_inc(folded_ready, 1)

            def add_bias(pair, kp, b):
                if b == 0:
                    pool.wait_ge(x_in[kp % 2], nth(pair, kp) * 16 + 16)
                tile = xr[:, kp % 2, b]
                nc.gpsimd.tensor_tensor(tile, tile, bias[:].unsqueeze(1).to_broadcast([P, T, E]),
                                        ALU.add).then_inc(x_ready, 1)

            def make_scale(g):
                pool.wait_ge(mean_ready, g + 1)
                wait(pool, result_ready, g)
                stand_apart(pool, passed_pool)
                nc.gpsimd.tensor_scalar(scale[:, 0, :], mean_var[:, :, 1], EPS, 1.0, ALU.add,
                                        ALU.mult).then_inc(var_added, 1)
                pool.wait_ge(var_added, g + 1)
                nc.gpsimd.tensor_tensor(scale[:, 2, :], scale[:, 0, :], scale[:, 1, :],
                                        ALU.pow).then_inc(sd_inverted, 1)
                pool.wait_ge(sd_inverted, 2 * g + 1)
                nc.gpsimd.tensor_tensor(scale[:, 3, :], mean_var[:, :, 0], scale[:, 2, :],
                                        ALU.mult).then_inc(sd_inverted, 1)
                pool.wait_ge(sd_inverted, 2 * g + 2)
                stand_apart(pool, passed_pool)
                nc.gpsimd.tensor_scalar(scale[:, 3, :], scale[:, 3, :], -1.0, 0.0, ALU.mult,
                                        ALU.add).then_inc(scale_ready, 1)

            nc.gpsimd.memset(ident[:], 0.0)
            nc.gpsimd.memset(draft, 0.0).then_inc(drafted, 1)
            pool.wait_ge(drafted, 1)
            nc.gpsimd.affine_select(out=ident[:], in_=ident[:], compare_op=ALU.not_equal, fill=1.0, base=0,
                                    pattern=[[-1, P]], channel_multiplier=1)
            nc.gpsimd.affine_select(out=draft, in_=draft, compare_op=ALU.not_equal, fill=1.0, base=0,
                                    pattern=[[-1, H], [0, P]], channel_multiplier=1).then_inc(drafted, 1)
            pool.wait_ge(drafted, 2)
            nc.gpsimd.affine_select(out=draft, in_=draft, compare_op=ALU.not_equal, fill=1.0, base=-LOW,
                                    pattern=[[-1, H], [0, P]], channel_multiplier=1).then_inc(drafted, 1)
            pool.wait_ge(cleared, 1)
            pool.wait_ge(drafted, 3)
            pool.memset(folded[:, 0, 0:1], 0.0).then_inc(constants, 1)
            pool.wait_ge(bias_ready, 1)

            def step(g, k):
                do = todo(g, k)
                for o in range(H):
                    if do["before"] and o == 1:
                        fold(g - 1, 3)
                    if do["cols"] and o in (3, 5, 7):
                        fold(g, (o - 3) // 2)
                    if do["kq"] and o in KQ_SLOTS:
                        low_kq(half(g, k, 3), (k + 3) // 2, KQ_SLOTS[o])
                    if do["second"] and o == 2:
                        make_scale(g - 2)
                    if do["cols"] and k % 2 == 0 and o in (4, 6):
                        add_bias(half(g, k, 0), k // 2, (o - 4) // 2)

            run_steps(pool, step)


def kernel(x, adj, L0_gnn_Wq, L0_gnn_bq, L0_gnn_Wk, L0_gnn_bk, L0_gnn_Wv, L0_gnn_bv, L0_gnn_Wo, L0_gnn_bo):
    import numpy as np
    import concourse.bacc as bacc
    from concourse.bass_utils import run_bass_kernel_spmd

    def rows_in(w):
        return np.ascontiguousarray(w.transpose().reshape(T, P, -1).transpose(1, 0, 2))

    def by_tile(w):
        return w.reshape(J, T, D, -1).transpose(1, 0, 2, 3).reshape(w.shape)

    def pairs(a, order):
        a = a.reshape(PAIRS, 2, T, P, -1).transpose((0, 3, 1, 2, 4) if order == "b t" else (0, 3, 2, 1, 4))
        return np.ascontiguousarray(a.reshape(PAIRS, P, -1))

    x, adj = np.asarray(x), np.asarray(adj)
    wq, wk, wv, wo = (np.asarray(w) for w in (L0_gnn_Wq, L0_gnn_Wk, L0_gnn_Wv, L0_gnn_Wo))
    bq, bk, bv, bo = (np.asarray(b) for b in (L0_gnn_bq, L0_gnn_bk, L0_gnn_bv, L0_gnn_bo))
    data = {
        "x": pairs(x, "b t"),
        "x_t": pairs(x.transpose(0, 2, 1), "t b"),
        "adj": pairs(adj, "b t"),
        "adj_t": pairs(adj.transpose(0, 2, 1), "b t"),
        "wq": rows_in(by_tile(wq)),
        "wk": rows_in(by_tile(wk)),
        "wv": rows_in(wv),
        "wo": rows_in(wo),
        "bq": np.ascontiguousarray(by_tile(bq).reshape(T, P).transpose()),
        "bk": np.ascontiguousarray(by_tile(bk).reshape(T, P).transpose()),
        "bv": np.ascontiguousarray(bv.reshape(T, P).transpose()),
        "bo": bo.reshape(1, E),
    }
    nc = bacc.Bacc("TRN2", target_bir_lowering=False, num_devices=1)
    args = [nc.dram_tensor(f"in_{n}", a.shape, F32, kind="ExternalInput").ap() for n, a in data.items()]
    out = nc.dram_tensor("out", (B, S, E), F32, kind="ExternalOutput").ap()
    build(nc, *args, out)
    r = run_bass_kernel_spmd(nc, [{f"in_{n}": a for n, a in data.items()}], core_ids=[0])
    return r.results[0]["out"]
```

```python
from contextlib import ExitStack

import concourse.bass as bass
from concourse import mybir
from concourse.alu_op_type import AluOpType as ALU

ACT = mybir.ActivationFunctionType
F32 = mybir.dt.float32
F32R = mybir.dt.float32r

P = 128
B, S, E = 32, 256, 256
H, D = 8, 32
T = S // P
J = P // D
PAIRS = B // 2
LOW = 64
ROWS = LOW + H
EPS = 1e-5
LOWEST = -3.4028234e38
BODY = 4
FIRST = 3
LOOPS = 6

KQ_SLOTS = {(0, 6): 0, (1, 1): 1, (1, 4): 2, (1, 6): 3}
V_SLOTS = {(0, 1): 0, (0, 4): 1}
X_SLOTS = {(0, 2): 0, (0, 3): 1}
TERMS = [(a, b, t) for a, b in ((0, 0), (0, 1), (1, 0)) for t in range(T)]
COLUMN_BANKS = 3
BANK_AGE = {0: 2, 1: 2, 2: 5}


def build(nc, x, x_t, adj, adj_t, wq, wk, wv, wo, bq, bk, bv, bo, out):
    ctx = ExitStack()
    with ctx:
        def sb(name, shape, dt=F32):
            return ctx.enter_context(nc.sbuf_tensor(name, shape, dt))

        def bank(name):
            return ctx.enter_context(nc.psum_tensor(name, [P, 512], F32))

        def sem(name):
            return ctx.enter_context(nc.semaphore(name))

        xt = sb("xt", [P, T, 2 * S])
        xt_parts = sb("xt_parts", [P, 2, 2, T, 2 * S], F32R)
        xr = sb("xr", [P, 2, 2, T, E])
        adj_rows = sb("adj_rows", [P, 2, 2, T, S])
        adj_cols = sb("adj_cols", [P, 2, 2, T, S])
        w_parts = sb("w_parts", [P, 2, 4, T, E], F32R)
        b_q, b_k, b_v = (sb(f"b_{n}", [P, T]) for n in "qkv")
        b_o = sb("b_o", [1, E])
        bias = sb("bias", [P, E])
        whole = sb("whole", [P, 2, 512])
        parts = sb("parts", [P, 4, T * 512], F32R)
        stack = sb("stack", [P, 2, 2, J, T * 512], F32R)
        v = sb("v", [P, 2, 2, T, E])
        top = sb("top", [P, 2, T, H])
        cut_top = sb("cut_top", [P, 2, T, ROWS], F32R)
        shift = sb("shift", [ROWS, S], F32R)
        pick = sb("pick", [ROWS, H, P], F32R)
        probs = sb("probs", [P, H, T * S])
        folded = sb("folded", [P, H, S])
        inverse = sb("inverse", [P, S])
        context = sb("context", [P, 2, S])
        ctx_parts = sb("ctx_parts", [P, 2, 2, S], F32R)
        y = sb("y", [P, T, E])
        stats = sb("stats", [P, T, 6])
        mean_var = sb("mean_var", [P, T, 2])
        scale = sb("scale", [P, 4, T])
        result = sb("result", [P, 2, T, E])
        ident = sb("ident", [P, P])
        ones = sb("ones", [P, P])
        w_whole = probs[:, 4:8, :].rearrange("p w (t e) -> p w t e", t=T)
        draft = probs[0:ROWS, 0:2, :].rearrange("p a (b k) -> p (a b) k", k=P)

        row_bank = [bank(f"row_bank{n}") for n in range(2)]
        col_bank = [bank(f"col_bank{n}") for n in range(COLUMN_BANKS)]
        ctx_bank = bank("ctx_bank")
        proj_bank = bank("proj_bank")
        out_bank = bank("out_bank")

        weights_in = sem("weights_in")
        x_in, adj_in, adj_t_in, stored = (
            [sem(f"{name}{n}") for n in range(2)] for name in ("x_in", "adj_in", "adj_t_in", "stored"))
        xt_in, xt_high, xt_low = sem("xt_in"), sem("xt_high"), sem("xt_low")
        w_high, w_cut = sem("w_high"), sem("w_cut")
        stacked = [[[sem(f"stacked{n}_{w}_{j}") for j in range(J)] for w in "kq"] for n in range(2)]
        cleared, drafted, constants = sem("cleared"), sem("drafted"), sem("constants")
        picked = sem("picked")
        bias_made, bias_ready = sem("bias_made"), sem("bias_ready")
        kq_made, kq_high, kq_low = sem("kq_made"), sem("kq_high"), sem("kq_low")
        v_made, v_ready = sem("v_made"), sem("v_ready")
        rows_made, rows_used = sem("rows_made"), sem("rows_used")
        top_high, top_cut, top_turned, shift_ready = (
            sem("top_high"), sem("top_cut"), sem("top_turned"), sem("shift_ready"))
        cols_made, masked, shifted, probs_ready = (
            sem("cols_made"), sem("masked"), sem("shifted"), sem("probs_ready"))
        folded_ready = sem("folded_ready")
        ctx_made, logs_ready, inverted, ctx_ready = sem("ctx_made"), sem("logs_ready"), sem("inverted"), sem("ctx_ready")
        ctx_high, ctx_low = sem("ctx_high"), sem("ctx_low")
        out_made, y_ready, stats_ready, mean_ready = (
            sem("out_made"), sem("y_ready"), sem("stats_ready"), sem("mean_ready"))
        var_added, sd_inverted, scale_ready = sem("var_added"), sem("sd_inverted"), sem("scale_ready")
        passed_dve, passed_pool = sem("passed_dve"), sem("passed_pool")
        x_ready, result_ready = sem("x_ready"), sem("result_ready")

        def flat(tile):
            return tile.rearrange("p a b c -> p (a b c)")

        out_d = out.rearrange("b (t p) e -> b p t e", p=P)

        def wait(eng, what, value):
            if not isinstance(value, int) or value > 0:
                eng.wait_ge(what, value)

        def head(pair, which, o, b):
            j, t = o // T, o % T
            return stack[:, pair % 2, which, j, t * 512 + b * S:t * 512 + (b + 1) * S]

        def stand_apart(eng, passed):
            eng.sem_inc(passed, 1)

        turn = []

        def run_steps(eng, step):
            for g in range(-4, FIRST):
                step(g, g)
            with eng.Fori(0, LOOPS) as u:
                turn.append(u)
                for k in range(FIRST, FIRST + BODY):
                    step(u * BODY + k, k)
            for g in range(FIRST + LOOPS * BODY, B + 2):
                step(g, g)

        def todo(g, k):
            loop = not isinstance(g, int)
            return {
                "rows": loop or 0 <= g + 1 < B,
                "cols": loop or 0 <= g < B,
                "before": loop or 0 <= g - 1 < B,
                "second": loop or 0 <= g - 2 < B,
                "kq": loop or 0 <= (g + 4) // 2 < PAIRS,
                "x": k % 2 == 0 and (loop or (g + 4) // 2 < PAIRS),
                "v": k % 2 == 0 and (loop or 0 <= (g + 2) // 2 < PAIRS),
            }

        def half(g, k, add):
            return (g + add) // 2 if isinstance(g, int) else turn[-1] * (BODY // 2) + (k + add) // 2

        def nth(pair, kp):
            return pair // 2 if isinstance(pair, int) else turn[-1] + kp // 2

        block = ctx.enter_context(nc.Block())

        @block.sync
        def _(sp):
            for n, dram in enumerate((wk, wq, wv, wo)):
                sp.dma_start(w_whole[:, n], dram).then_inc(weights_in, 16)
            for tile, dram in ((b_q, bq), (b_k, bk), (b_v, bv), (b_o, bo)):
                sp.dma_start(tile[:], dram).then_inc(weights_in, 16)
            sp.dma_start(xt[:].rearrange("p t s -> p (t s)"), x_t[0]).then_inc(xt_in, 16)

            def step(g, k):
                if k % 2 == 0 or not todo(g, k)["kq"]:
                    return
                pair, kp = half(g, k, 3), (k + 3) // 2
                if not isinstance(g, int) or g + 5 < 2 * PAIRS:
                    wait(sp, xt_low, 2 * pair + 2)
                    sp.dma_start(xt[:].rearrange("p t s -> p (t s)"), x_t[pair + 1]).then_inc(xt_in, 16)
                for which in range(2):
                    wait(sp, kq_low, 4 * pair + 2 * which + 2)
                    for j in range(J):
                        wait(sp, cols_made, 8 * g + 2 * j + 2)
                        for group in range(J):
                            part = group % 2 if which == 0 else group // 2
                            sp.dma_start(stack[D * group:D * (group + 1), kp % 2, which, j, :].bitcast(F32),
                                         parts[D * j:D * (j + 1), 2 * which + part, :].bitcast(F32)
                                         ).then_inc(stacked[kp % 2][which][j], 16)

            run_steps(sp, step)

        @block.tensor
        def _(pe):
            def rows(n, kn, o):
                if o % T == 0:
                    for which in range(2):
                        pe.wait_ge(stacked[(kn // 2) % 2][which][o // T],
                                   nth(half(n, kn, -(kn % 2)), kn // 2) * (J * 16) + J * 16)
                wait(pe, rows_used, 8 * n + o - 1)
                q, key = head(kn // 2, 1, o, kn % 2), head(kn // 2, 0, o, kn % 2)
                for t in range(T):
                    last = nc.tensor.matmul(row_bank[o % 2][:, t * S:(t + 1) * S], q[:, t * P:(t + 1) * P], key,
                                            start=(t == 0), stop=True, skip_group_check=True)
                last.then_inc(rows_made, 1)

            def cols(g, k, o):
                wait(pe, probs_ready, 8 * g + o - BANK_AGE.get(o, COLUMN_BANKS) + 1)
                q, key = head(k // 2, 1, o, k % 2), head(k // 2, 0, o, k % 2)
                for t in range(T):
                    last = nc.tensor.matmul(col_bank[o % COLUMN_BANKS][:, t * S:(t + 1) * S],
                                            key[:, t * P:(t + 1) * P], q,
                                            start=(t == 0), stop=True, skip_group_check=True)
                last.then_inc(cols_made, 1)

            def subtract_top(g, o):
                if o == 0:
                    pe.wait_ge(shift_ready, g + 1)
                pe.wait_ge(masked, 8 * g + o + 1)
                nc.tensor.matmul(col_bank[o % COLUMN_BANKS][:], pick[:, o, :],
                                 shift[:].unsqueeze(1).to_broadcast([ROWS, T, S]),
                                 start=False, stop=True, skip_group_check=True).then_inc(shifted, 1)

            def turn_top(g, k):
                pe.wait_ge(top_cut, g + 1)
                before = half(g, k, 2) * 4 + 4 if k % 2 == 0 else half(g, k, 3) * 4 + 1
                pe.wait_ge(kq_high, min(before, 4 * PAIRS) if isinstance(before, int) else before)
                for t in range(T):
                    last = nc.tensor.transpose(proj_bank[0:ROWS, t * P:(t + 1) * P],
                                               cut_top[:, k % 2, t, :].bitcast(F32), ident[:])
                last.then_inc(top_turned, 1)

            def project_kq(pair, kp, c):
                if c == 0:
                    pe.wait_ge(xt_low, 2 * pair + 2)
                    wait(pe, v_ready, 2 * pair)
                else:
                    pe.wait_ge(kq_high, 4 * pair + c)
                if c == 1:
                    wait(pe, shift_ready, 2 * pair - 2)
                features = slice((c % 2) * P, (c % 2 + 1) * P)
                for n, (a, b, t) in enumerate(TERMS):
                    last = nc.tensor.matmul(proj_bank[:], w_parts[:, a, c // 2, t, features],
                                            xt_parts[:, kp % 2, b, t, :],
                                            start=(n == 0), stop=(n == len(TERMS) - 1))
                last.then_inc(kq_made, 1)

            def project_v(pair, kp, b):
                if b == 0:
                    pe.wait_ge(kq_high, 4 * pair + 4)
                    wait(pe, shift_ready, 2 * pair - 1)
                else:
                    pe.wait_ge(v_ready, 2 * pair + 1)
                for n in range(T):
                    nodes = slice(b * S + n * P, b * S + (n + 1) * P)
                    for i, (a, c, t) in enumerate(TERMS):
                        last = nc.tensor.matmul(proj_bank[:, n * E:(n + 1) * E], xt_parts[:, kp % 2, a, t, nodes],
                                                w_parts[:, c, 2, t, :], start=(n == 0 and i == 0),
                                                stop=(i == len(TERMS) - 1), skip_group_check=True)
                last.then_inc(v_made, 1)

            def weigh_v(g, k, half_):
                if half_ == 0:
                    pe.wait_ge(v_ready, g + 1)
                wait(pe, ctx_ready, 2 * g + half_)
                pe.wait_ge(folded_ready, 4 * g + 2 * half_ + 2)
                heads = range(J * half_, J * half_ + J)
                for t in range(T):
                    for o in heads:
                        c = D * (o % J)
                        nc.tensor.matmul(ctx_bank[c:c + D, 0:S], v[:, (k // 2) % 2, k % 2, t, o * D:(o + 1) * D],
                                         probs[:, o, t * S:(t + 1) * S], start=(t == 0), stop=(t == T - 1),
                                         tile_position=(0, c))
                for o in heads:
                    c = D * (o % J)
                    last = nc.tensor.matmul(ctx_bank[c:c + D, S:2 * S], ones[:, 0:D], folded[:, o, :],
                                            start=True, stop=True, tile_position=(0, c))
                last.then_inc(ctx_made, 1)

            def project_out(g):
                pe.wait_ge(ctx_low, 2 * g + 2)
                wait(pe, y_ready, g)
                for n in range(T):
                    nodes = slice(n * P, (n + 1) * P)
                    for i, (a, b, f) in enumerate(TERMS):
                        last = nc.tensor.matmul(out_bank[:, n * E:(n + 1) * E], ctx_parts[:, a, f, nodes],
                                                w_parts[:, b, 3, f, :], start=(n == 0 and i == 0),
                                                stop=(i == len(TERMS) - 1), skip_group_check=True)
                last.then_inc(out_made, 1)

            pe.wait_ge(constants, 1)
            pe.wait_ge(weights_in, 8 * 16)
            nc.tensor.matmul(out_bank[:, 0:E], ones[0:1, :], b_o[:], start=True, stop=False)
            for f in range(T):
                last = nc.tensor.matmul(out_bank[:, 0:E], b_v[:, f:f + 1].to_broadcast([P, P]), w_whole[:, 3, f, :],
                                        start=False, stop=(f == T - 1))
            last.then_inc(bias_made, 1)
            pe.wait_ge(bias_ready, 1)
            pe.wait_ge(picked, 1)
            pe.wait_ge(w_cut, 1)

            def step(g, k):
                do = todo(g, k)
                for o in range(H):
                    if do["rows"]:
                        rows(g + 1, k + 1, o)
                    if do["cols"]:
                        cols(g, k, o)
                    if do["kq"] and (k % 2, o) in KQ_SLOTS:
                        project_kq(half(g, k, 3 + (k + 1) % 2), (k + 4) // 2, KQ_SLOTS[k % 2, o])
                    if do["v"] and (k % 2, o) in V_SLOTS:
                        project_v(half(g, k, 2), (k + 2) // 2, V_SLOTS[k % 2, o])
                    if o == 3 and do["before"]:
                        weigh_v(g - 1, k - 1, 1)
                    if o == 0 and do["second"]:
                        project_out(g - 2)
                    if o == 7 and do["cols"]:
                        weigh_v(g, k, 0)
                    if o == 0:
                        if do["before"]:
                            subtract_top(g - 1, H - 1)
                        if do["cols"]:
                            turn_top(g, k)
                    elif do["cols"]:
                        subtract_top(g, o - 1)

            run_steps(pe, step)

        @block.vector
        def _(dve):
            def reduce_rows(n, kn, o):
                if o == 0:
                    dve.wait_ge(adj_in[(kn // 2) % 2], nth(half(n, kn, -(kn % 2)), kn // 2) * 16 + 16)
                dve.wait_ge(rows_made, 8 * n + o + 1)
                stand_apart(dve, passed_dve)
                for t in range(T):
                    tile = row_bank[o % 2][:, t * S:(t + 1) * S]
                    last = nc.vector.tensor_tensor_reduce(
                        tile, tile, adj_rows[:, (kn // 2) % 2, kn % 2, t, :], 1.0, LOWEST, ALU.mult, ALU.max,
                        top[:, kn % 2, t, o:o + 1])
                last.then_inc(rows_used, 1)

            def cut_tops(n, kn):
                dve.wait_ge(rows_used, 8 * n + 8)
                high, low = cut_top[:, kn % 2, :, 0:H], cut_top[:, kn % 2, :, LOW:ROWS]
                nc.vector.tensor_scalar(high, top[:, kn % 2], -1.0, None, ALU.mult).then_inc(top_high, 1)
                dve.wait_ge(top_high, n + 1)
                nc.vector.scalar_tensor_tensor(low, top[:, kn % 2], -1.0, high.bitcast(F32),
                                               ALU.mult, ALU.subtract).then_inc(top_cut, 1)

            def mask_cols(g, k, o):
                if o == 0:
                    dve.wait_ge(adj_t_in[(k // 2) % 2], nth(half(g, k, -(k % 2)), k // 2) * 16 + 16)
                dve.wait_ge(cols_made, 8 * g + o + 1)
                tile = col_bank[o % COLUMN_BANKS][:]
                nc.vector.tensor_tensor(tile, tile, adj_cols[:, (k // 2) % 2, k % 2].rearrange("p t s -> p (t s)"),
                                        ALU.mult).then_inc(masked, 1)

            def scale_context(g, half_):
                dve.wait_ge(inverted, 2 * g + half_ + 1)
                wait(dve, ctx_low, 2 * g + half_ - 1)
                nc.vector.tensor_tensor(context[:, half_, :], ctx_bank[:, 0:S], inverse[:],
                                        ALU.mult).then_inc(ctx_ready, 1)

            def add_residual(g, k):
                dve.wait_ge(out_made, g + 1)
                dve.wait_ge(x_ready, g + 1)
                wait(dve, result_ready, g)
                nc.vector.tensor_tensor(y[:].rearrange("p t e -> p (t e)"), out_bank[:],
                                        xr[:, (k // 2) % 2, k % 2].rearrange("p t e -> p (t e)"),
                                        ALU.add).then_inc(y_ready, 1)

            def row_stats(g):
                dve.wait_ge(y_ready, g + 1)
                for t in range(T):
                    last = nc.vector.bn_stats(stats[:, t, :], y[:, t, :])
                last.then_inc(stats_ready, 1)

            def aggregate(g):
                dve.wait_ge(stats_ready, g + 1)
                wait(dve, scale_ready, g)
                stand_apart(dve, passed_dve)
                for t in range(T):
                    last = nc.vector.bn_aggr(mean_var[:, t, :], stats[:, t, :])
                last.then_inc(mean_ready, 1)

            nc.vector.memset(cut_top[:].bitcast(F32), 0.0)
            nc.vector.memset(scale[:, 1, :], -0.5)
            nc.vector.memset(ones[:], 1.0).then_inc(cleared, 1)
            dve.wait_ge(cleared, 1)
            dve.wait_ge(drafted, 3)
            nc.vector.tensor_copy(pick[:], draft).then_inc(picked, 1)
            dve.wait_ge(weights_in, 8 * 16)
            high = w_parts[:, 0].rearrange("p w t e -> p (w t e)")
            whole_w = probs[:, 4:8, :].rearrange("p w e -> p (w e)")
            nc.vector.tensor_copy(high, whole_w).then_inc(w_high, 1)
            dve.wait_ge(w_high, 1)
            nc.vector.tensor_tensor(w_parts[:, 1].rearrange("p w t e -> p (w t e)"), whole_w, high.bitcast(F32),
                                    ALU.subtract).then_inc(w_cut, 1)
            dve.wait_ge(bias_made, 1)
            nc.vector.tensor_copy(bias[:], out_bank[:, 0:E]).then_inc(bias_ready, 1)

            def step(g, k):
                do = todo(g, k)
                for o in range(H):
                    if do["rows"]:
                        reduce_rows(g + 1, k + 1, o)
                        if o == H - 1:
                            cut_tops(g + 1, k + 1)
                    if do["cols"]:
                        mask_cols(g, k, o)
                    if do["before"]:
                        if o == 1:
                            scale_context(g - 1, 0)
                        if o == 5:
                            scale_context(g - 1, 1)
                    if do["second"]:
                        if o == 2:
                            add_residual(g - 2, k - 2)
                        if o == 3:
                            row_stats(g - 2)
                        if o == 4:
                            aggregate(g - 2)

            run_steps(dve, step)

        @block.scalar
        def _(act):
            def load_masks(pair, kp):
                wait(act, masked, 16 * (pair - 1))
                act.dma_start(flat(adj_rows[:, kp % 2]), adj[pair]).then_inc(adj_in[kp % 2], 16)
                act.dma_start(flat(adj_cols[:, kp % 2]), adj_t[pair]).then_inc(adj_t_in[kp % 2], 16)

            def load_x(pair, kp):
                wait(act, y_ready, 2 * (pair - 1))
                act.dma_start(flat(xr[:, kp % 2]), x[pair]).then_inc(x_in[kp % 2], 16)

            def exp(g, k, o):
                act.wait_ge(shifted, 8 * g + o + 1)
                if o % J == 0:
                    wait(act, ctx_made, 2 * g - 1 + o // J)
                nc.scalar.activation(probs[:, o, :], col_bank[o % COLUMN_BANKS][:], ACT.Exp,
                                     scale=2.0 * float(D) ** -0.5).then_inc(probs_ready, 1)

            def invert(g, half_):
                act.wait_ge(ctx_made, 2 * g + half_ + 1)
                wait(act, ctx_ready, 2 * g + half_)
                nc.scalar.activation(inverse[:], ctx_bank[:, S:2 * S], ACT.Ln).then_inc(logs_ready, 1)
                act.wait_ge(logs_ready, 2 * g + half_ + 1)
                nc.scalar.activation(inverse[:], inverse[:], ACT.Exp, scale=-1.0).then_inc(inverted, 1)

            def cut_context(g, half_):
                act.wait_ge(ctx_ready, 2 * g + half_ + 1)
                wait(act, out_made, g)
                nc.scalar.copy(ctx_parts[:, 0, half_, :], context[:, half_, :]).then_inc(ctx_high, 1)

            def cut_x(pair, kp, t):
                if t == 0:
                    act.wait_ge(xt_in, 16 * pair + 16)
                    wait(act, v_made, 2 * pair - 2)
                nc.scalar.copy(xt_parts[:, kp % 2, 0, t, :], xt[:, t, :]).then_inc(xt_high, 1)

            def copy_shift(g):
                act.wait_ge(top_turned, g + 1)
                nc.scalar.copy(shift[:], out_bank[0:ROWS, 0:S]).then_inc(shift_ready, 1)

            def cut_kq(pair, kp, c):
                act.wait_ge(kq_made, 4 * pair + c + 1)
                wait(act, kq_low, 4 * pair + c - 1)
                if c % 2 == 0:
                    last = pair - 1
                    for j in range(J):
                        wait(act, stacked[(kp - 1) % 2][c // 2][j], nth(last, kp - 1) * (J * 16) + J * 16
                             if not isinstance(pair, int) or pair > 0 else 0)
                b = (b_k if c < 2 else b_q)[:, c % 2:c % 2 + 1]
                nc.scalar.activation(whole[:, c % 2, :], proj_bank[:], ACT.Identity, bias=b)
                nc.scalar.activation(parts[:, 2 * (c // 2), (c % 2) * 512:(c % 2 + 1) * 512],
                                     proj_bank[:], ACT.Identity, bias=b).then_inc(kq_high, 1)

            def copy_v(pair, kp, b):
                act.wait_ge(v_made, 2 * pair + b + 1)
                nc.scalar.copy(v[:, kp % 2, b].rearrange("p t e -> p (t e)"), proj_bank[:]).then_inc(v_ready, 1)

            def normalise(g, k):
                act.wait_ge(scale_ready, g + 1)
                act.wait_ge(stored[k % 2], half(g, k, -(k % 2)) * 16 + 16)
                for t in range(T):
                    last = nc.scalar.activation(result[:, k % 2, t, :], y[:, t, :], ACT.Identity,
                                                bias=scale[:, 3, t:t + 1], scale=scale[:, 2, t:t + 1])
                last.then_inc(result_ready, 1)

            def store(g, k):
                act.wait_ge(result_ready, g + 1)
                act.dma_start(out_d[g], result[:, k % 2]).then_inc(stored[k % 2], 16)

            for n in range(2):
                act.sem_inc(stored[n], 16)
            nc.scalar.preload_act_table_set("natural_log_exp_and_others")
            act.wait_ge(weights_in, 8 * 16)
            act.wait_ge(picked, 1)
            act.wait_ge(w_cut, 1)

            def step(g, k):
                do = todo(g, k)
                for o in range(H):
                    if o == 0:
                        if do["before"]:
                            exp(g - 1, k - 1, H - 1)
                        if do["cols"]:
                            copy_shift(g)
                        if do["v"]:
                            load_masks(half(g, k, 2), (k + 2) // 2)
                    elif do["cols"]:
                        exp(g, k, o - 1)
                    if o == 4 and k % 2 == 1 and do["rows"]:
                        load_x(half(g, k, 1), (k + 1) // 2)
                    if do["kq"] and (k % 2, o) in KQ_SLOTS:
                        cut_kq(half(g, k, 3 + (k + 1) % 2), (k + 4) // 2, KQ_SLOTS[k % 2, o])
                    if do["v"] and (k % 2, o) in V_SLOTS:
                        copy_v(half(g, k, 2), (k + 2) // 2, V_SLOTS[k % 2, o])
                    if do["x"] and (k % 2, o) in X_SLOTS:
                        cut_x(half(g, k, 4), (k + 4) // 2, X_SLOTS[k % 2, o])
                    if do["before"] and o in (0, 4):
                        invert(g - 1, o // 4)
                    if do["before"] and o in (2, 6):
                        cut_context(g - 1, o // 4)
                    if do["second"]:
                        if o == 6:
                            normalise(g - 2, k - 2)
                        if o == 7:
                            store(g - 2, k - 2)

            run_steps(act, step)
            for n in range(2):
                act.wait_ge(stored[n], 16 * (B // 2) + 16)

        @block.gpsimd
        def _(pool):
            def low_kq(pair, kp, c):
                pool.wait_ge(kq_high, 4 * pair + c + 1)
                cut = slice((c % 2) * 512, (c % 2 + 1) * 512)
                nc.gpsimd.tensor_tensor(parts[:, 2 * (c // 2) + 1, cut], whole[:, c % 2, :],
                                        parts[:, 2 * (c // 2), cut].bitcast(F32),
                                        ALU.subtract).then_inc(kq_low, 1)

            def low_x(pair, kp, t):
                pool.wait_ge(xt_high, 2 * pair + t + 1)
                nc.gpsimd.tensor_tensor(xt_parts[:, kp % 2, 1, t, :], xt[:, t, :], xt_parts[:, kp % 2, 0, t, :].bitcast(F32),
                                        ALU.subtract).then_inc(xt_low, 1)

            def low_context(g, half_):
                pool.wait_ge(ctx_high, 2 * g + half_ + 1)
                nc.gpsimd.tensor_tensor(ctx_parts[:, 1, half_, :], context[:, half_, :],
                                        ctx_parts[:, 0, half_, :].bitcast(F32), ALU.subtract).then_inc(ctx_low, 1)

            def fold(g, i):
                pool.wait_ge(probs_ready, 8 * g + 2 * i + 2)
                wait(pool, ctx_made, 2 * g - 1 + i // 2)
                nc.gpsimd.tensor_tensor(folded[:, 2 * i:2 * i + 2, :], probs[:, 2 * i:2 * i + 2, 0:S],
                                        probs[:, 2 * i:2 * i + 2, S:2 * S], ALU.add).then_inc(folded_ready, 1)

            def add_bias(pair, kp, b):
                if b == 0:
                    pool.wait_ge(x_in[kp % 2], nth(pair, kp) * 16 + 16)
                tile = xr[:, kp % 2, b]
                nc.gpsimd.tensor_tensor(tile, tile, bias[:].unsqueeze(1).to_broadcast([P, T, E]),
                                        ALU.add).then_inc(x_ready, 1)

            def make_scale(g):
                pool.wait_ge(mean_ready, g + 1)
                wait(pool, result_ready, g)
                stand_apart(pool, passed_pool)
                nc.gpsimd.tensor_scalar(scale[:, 0, :], mean_var[:, :, 1], EPS, 1.0, ALU.add,
                                        ALU.mult).then_inc(var_added, 1)
                pool.wait_ge(var_added, g + 1)
                nc.gpsimd.tensor_tensor(scale[:, 2, :], scale[:, 0, :], scale[:, 1, :],
                                        ALU.pow).then_inc(sd_inverted, 1)
                pool.wait_ge(sd_inverted, 2 * g + 1)
                nc.gpsimd.tensor_tensor(scale[:, 3, :], mean_var[:, :, 0], scale[:, 2, :],
                                        ALU.mult).then_inc(sd_inverted, 1)
                pool.wait_ge(sd_inverted, 2 * g + 2)
                stand_apart(pool, passed_pool)
                nc.gpsimd.tensor_scalar(scale[:, 3, :], scale[:, 3, :], -1.0, 0.0, ALU.mult,
                                        ALU.add).then_inc(scale_ready, 1)

            nc.gpsimd.memset(ident[:], 0.0)
            nc.gpsimd.memset(draft, 0.0).then_inc(drafted, 1)
            pool.wait_ge(drafted, 1)
            nc.gpsimd.affine_select(out=ident[:], in_=ident[:], compare_op=ALU.not_equal, fill=1.0, base=0,
                                    pattern=[[-1, P]], channel_multiplier=1)
            nc.gpsimd.affine_select(out=draft, in_=draft, compare_op=ALU.not_equal, fill=1.0, base=0,
                                    pattern=[[-1, H], [0, P]], channel_multiplier=1).then_inc(drafted, 1)
            pool.wait_ge(drafted, 2)
            nc.gpsimd.affine_select(out=draft, in_=draft, compare_op=ALU.not_equal, fill=1.0, base=-LOW,
                                    pattern=[[-1, H], [0, P]], channel_multiplier=1).then_inc(drafted, 1)
            pool.wait_ge(cleared, 1)
            pool.wait_ge(drafted, 3)
            pool.memset(folded[:, 0, 0:1], 0.0).then_inc(constants, 1)
            pool.wait_ge(bias_ready, 1)

            def step(g, k):
                do = todo(g, k)
                for o in range(H):
                    if do["before"] and o == 0:
                        fold(g - 1, 3)
                    if do["x"] and (k % 2, o) in X_SLOTS:
                        low_x(half(g, k, 4), (k + 4) // 2, X_SLOTS[k % 2, o])
                    if do["before"] and o in (2, 6):
                        low_context(g - 1, o // 4)
                    if do["cols"] and o in (3, 5, 7):
                        fold(g, (o - 3) // 2)
                    if do["kq"] and (k % 2, o) in KQ_SLOTS:
                        low_kq(half(g, k, 3 + (k + 1) % 2), (k + 4) // 2, KQ_SLOTS[k % 2, o])
                    if do["second"] and o == 5:
                        make_scale(g - 2)
                    if do["cols"] and k % 2 == 0 and o in (4, 6):
                        add_bias(half(g, k, 0), k // 2, (o - 4) // 2)

            run_steps(pool, step)


def kernel(x, adj, L0_gnn_Wq, L0_gnn_bq, L0_gnn_Wk, L0_gnn_bk, L0_gnn_Wv, L0_gnn_bv, L0_gnn_Wo, L0_gnn_bo):
    import numpy as np
    import concourse.bacc as bacc
    from concourse.bass_utils import run_bass_kernel_spmd

    def rows_in(w):
        return np.ascontiguousarray(w.transpose().reshape(T, P, -1).transpose(1, 0, 2))

    def by_tile(w):
        return w.reshape(J, T, D, -1).transpose(1, 0, 2, 3).reshape(w.shape)

    def pairs(a, order):
        a = a.reshape(PAIRS, 2, T, P, -1).transpose((0, 3, 1, 2, 4) if order == "b t" else (0, 3, 2, 1, 4))
        return np.ascontiguousarray(a.reshape(PAIRS, P, -1))

    x, adj = np.asarray(x), np.asarray(adj)
    wq, wk, wv, wo = (np.asarray(w) for w in (L0_gnn_Wq, L0_gnn_Wk, L0_gnn_Wv, L0_gnn_Wo))
    bq, bk, bv, bo = (np.asarray(b) for b in (L0_gnn_bq, L0_gnn_bk, L0_gnn_bv, L0_gnn_bo))
    data = {
        "x": pairs(x, "b t"),
        "x_t": pairs(x.transpose(0, 2, 1), "t b"),
        "adj": pairs(adj, "b t"),
        "adj_t": pairs(adj.transpose(0, 2, 1), "b t"),
        "wq": rows_in(by_tile(wq)),
        "wk": rows_in(by_tile(wk)),
        "wv": rows_in(wv),
        "wo": rows_in(wo),
        "bq": np.ascontiguousarray(by_tile(bq).reshape(T, P).transpose()),
        "bk": np.ascontiguousarray(by_tile(bk).reshape(T, P).transpose()),
        "bv": np.ascontiguousarray(bv.reshape(T, P).transpose()),
        "bo": bo.reshape(1, E),
    }
    nc = bacc.Bacc("TRN2", target_bir_lowering=False, num_devices=1)
    args = [nc.dram_tensor(f"in_{n}", a.shape, F32, kind="ExternalInput").ap() for n, a in data.items()]
    out = nc.dram_tensor("out", (B, S, E), F32, kind="ExternalOutput").ap()
    build(nc, *args, out)
    r = run_bass_kernel_spmd(nc, [{f"in_{n}": a for n, a in data.items()}], core_ids=[0])
    return r.results[0]["out"]
```

```python
from contextlib import ExitStack

import concourse.bass as bass
from concourse import mybir
from concourse.alu_op_type import AluOpType as ALU

ACT = mybir.ActivationFunctionType
F32 = mybir.dt.float32
F32R = mybir.dt.float32r

P = 128
B, S, E = 32, 256, 256
H, D = 8, 32
T = S // P
J = P // D
PAIRS = B // 2
LOW = 64
ROWS = LOW + H
EPS = 1e-5
LOWEST = -3.4028234e38
BODY = 4
FIRST = 3
LOOPS = 6

KQ_SLOTS = {(0, 4): (0, 0), (0, 5): (0, 1), (0, 6): (1, 0), (1, 0): (1, 1),
            (1, 2): (2, 0), (1, 3): (2, 1), (1, 5): (3, 0), (1, 7): (3, 1)}
KQ_CUT_SLOTS = {(0, 5): 0, (1, 1): 1, (1, 4): 2, (1, 7): 3}
OUT_SLOTS = {(0, 5): 0, (0, 6): 1, (1, 4): 0, (1, 5): 1}
X_SLOTS = {(0, 0): 0, (0, 1): 1}
TERMS = [(a, b, t) for a, b in ((0, 0), (0, 1), (1, 0)) for t in range(T)]
COLUMN_BANKS = 3


def build(nc, x, x_t, adj, adj_t, wq, wk, wv, wo, bq, bk, bv, bo, out):
    ctx = ExitStack()
    with ctx:
        def sb(name, shape, dt=F32):
            return ctx.enter_context(nc.sbuf_tensor(name, shape, dt))

        def bank(name):
            return ctx.enter_context(nc.psum_tensor(name, [P, 512], F32))

        def sem(name):
            return ctx.enter_context(nc.semaphore(name))

        xt = sb("xt", [P, T, 2 * S])
        xt_parts = sb("xt_parts", [P, 2, 2, T, 2 * S], F32R)
        xr = sb("xr", [P, 2, 2, T, E])
        adj_rows = sb("adj_rows", [P, 2, 2, T, S])
        adj_cols = sb("adj_cols", [P, 2, 2, T, S])
        w_parts = sb("w_parts", [P, 2, 4, T, E], F32R)
        b_q, b_k, b_v = (sb(f"b_{n}", [P, T]) for n in "qkv")
        b_o = sb("b_o", [1, E])
        bias = sb("bias", [P, E])
        whole = sb("whole", [P, 2, 512])
        parts = sb("parts", [P, 4, T * 512], F32R)
        stack = sb("stack", [P, 2, 2, J, T * 512], F32R)
        v = sb("v", [P, 2, 2, T, E])
        top = sb("top", [P, 2, T, H])
        cut_top = sb("cut_top", [P, 2, T, ROWS], F32R)
        shift = sb("shift", [ROWS, 2, S], F32R)
        pick = sb("pick", [ROWS, H, P], F32R)
        probs = sb("probs", [P, H, T * S])
        folded = sb("folded", [P, H, S])
        inverse = sb("inverse", [P, S])
        context = sb("context", [P, 2, S])
        ctx_parts = sb("ctx_parts", [P, 2, 2, 2, S], F32R)
        y = sb("y", [P, T, E])
        stats = sb("stats", [P, T, 6])
        mean_var = sb("mean_var", [P, T, 2])
        scale = sb("scale", [P, 4, T])
        result = sb("result", [P, 2, T, E])
        ident = sb("ident", [P, P])
        ones = sb("ones", [P, P])
        w_whole = probs[:, 4:8, :].rearrange("p w (t e) -> p w t e", t=T)
        draft = probs[0:ROWS, 0:2, :].rearrange("p a (b k) -> p (a b) k", k=P)

        row_bank = [bank(f"row_bank{n}") for n in range(2)]
        col_bank = [bank(f"col_bank{n}") for n in range(COLUMN_BANKS)]
        ctx_bank = bank("ctx_bank")
        proj_bank = bank("proj_bank")
        out_bank = bank("out_bank")

        weight_in = [sem(f"weight_in_{n}") for n in "kqvo"]
        biases_in = sem("biases_in")
        x_in, adj_in, adj_t_in, stored = (
            [sem(f"{name}{n}") for n in range(2)] for name in ("x_in", "adj_in", "adj_t_in", "stored"))
        xt_in, xt_high, xt_low = sem("xt_in"), sem("xt_high"), sem("xt_low")
        w_high, w_cut = sem("w_high"), sem("w_cut")
        stacked = [[[sem(f"stacked{n}_{w}_{j}") for j in range(J)] for w in "kq"] for n in range(2)]
        cleared, drafted, constants = sem("cleared"), sem("drafted"), sem("constants")
        picked = sem("picked")
        bias_made, bias_ready = sem("bias_made"), sem("bias_ready")
        kq_made, kq_high, kq_low = sem("kq_made"), sem("kq_high"), sem("kq_low")
        v_made, v_ready = sem("v_made"), sem("v_ready")
        rows_made, rows_used = sem("rows_made"), sem("rows_used")
        top_high, top_cut, top_turned, shift_ready = (
            sem("top_high"), sem("top_cut"), sem("top_turned"), sem("shift_ready"))
        cols_made, masked, shifted, probs_ready = (
            sem("cols_made"), sem("masked"), sem("shifted"), sem("probs_ready"))
        folded_ready = sem("folded_ready")
        ctx_made, logs_ready, inverted, ctx_ready = (
            sem("ctx_made"), sem("logs_ready"), sem("inverted"), sem("ctx_ready"))
        ctx_high, ctx_low = sem("ctx_high"), sem("ctx_low")
        out_made, y_ready, stats_ready, mean_ready = (
            sem("out_made"), sem("y_ready"), sem("stats_ready"), sem("mean_ready"))
        var_added, sd_inverted, scale_ready = sem("var_added"), sem("sd_inverted"), sem("scale_ready")
        passed_dve, passed_pool = sem("passed_dve"), sem("passed_pool")
        x_ready, result_ready = sem("x_ready"), sem("result_ready")

        def flat(tile):
            return tile.rearrange("p a b c -> p (a b c)")

        out_d = out.rearrange("b (t p) e -> b p t e", p=P)

        def wait(eng, what, value):
            if not isinstance(value, int) or value > 0:
                eng.wait_ge(what, value)

        def head(pair, which, o, b):
            j, t = o // T, o % T
            return stack[:, pair % 2, which, j, t * 512 + b * S:t * 512 + (b + 1) * S]

        def bank_slot(k, o):
            return (k - FIRST) % BODY * H + o

        def col(k, o):
            return col_bank[bank_slot(k, o) % COLUMN_BANKS]

        def context_bank(g, half_):
            return row_bank[0] if isinstance(g, int) and g == B - 1 and half_ == 1 else ctx_bank

        def kq_bank(pair, c):
            if isinstance(pair, int) and pair < 2:
                return ((row_bank[0], row_bank[1], col_bank[0], proj_bank), (proj_bank, *col_bank))[pair][c]
            return proj_bank

        def stack_first(eng, copy, which, j):
            eng.wait_ge(kq_low, 2 * which + 2)
            for group in range(J):
                part = group % 2 if which == 0 else group // 2
                copy(stack[D * group:D * (group + 1), 0, which, j, :],
                     parts[D * j:D * (j + 1), 2 * which + part, :]).then_inc(stacked[0][which][j], 16)

        def stand_apart(eng, passed):
            eng.sem_inc(passed, 1)

        turn = []

        def run_steps(eng, step):
            for g in range(-4, FIRST):
                step(g, g)
            with eng.Fori(0, LOOPS) as u:
                turn.append(u)
                for k in range(FIRST, FIRST + BODY):
                    step(u * BODY + k, k)
            for g in range(FIRST + LOOPS * BODY, B + 3):
                step(g, g)

        def todo(g, k):
            loop = not isinstance(g, int)
            return {
                "rows": loop or 0 <= g + 1 < B,
                "next rows": loop or 0 <= g + 2 < B,
                "cols": loop or 0 <= g < B,
                "before": loop or 0 <= g - 1 < B,
                "second": loop or 0 <= g - 2 < B,
                "third": loop or 0 <= g - 3 < B,
                "kq": loop or 0 <= (g + 4) // 2 < PAIRS,
                "x": k % 2 == 0 and (loop or (g + 4) // 2 < PAIRS),
                "v": loop or 0 <= g + 2 < B,
            }

        def half(g, k, add):
            return (g + add) // 2 if isinstance(g, int) else turn[-1] * (BODY // 2) + (k + add) // 2

        def nth(pair, kp):
            return pair // 2 if isinstance(pair, int) else turn[-1] + kp // 2

        block = ctx.enter_context(nc.Block())

        @block.sync
        def _(sp):
            sp.dma_start(xt[:].rearrange("p t s -> p (t s)"), x_t[0]).then_inc(xt_in, 16)
            for n, dram in enumerate((wk, wq, wv, wo)):
                sp.dma_start(w_whole[:, n], dram).then_inc(weight_in[n], 16)
                if n == 0:
                    for tile, bias_dram in ((b_k, bk), (b_q, bq)):
                        sp.dma_start(tile[:], bias_dram).then_inc(biases_in, 16)
            for tile, dram in ((b_v, bv), (b_o, bo)):
                sp.dma_start(tile[:], dram).then_inc(biases_in, 16)

            def step(g, k):
                if k % 2 == 0 or not todo(g, k)["kq"]:
                    return
                pair, kp = half(g, k, 3), (k + 3) // 2
                if not isinstance(g, int) or g + 5 < 2 * PAIRS:
                    wait(sp, xt_low, 2 * pair + 2)
                    sp.dma_start(xt[:].rearrange("p t s -> p (t s)"), x_t[pair + 1]).then_inc(xt_in, 16)
                for which in range(1 if k == -3 else 2):
                    wait(sp, kq_low, 4 * pair + 2 * which + 2)
                    for j in range(J - 1 if k == -3 else J):
                        wait(sp, cols_made, 8 * g + 2 * j + 2)
                        for group in range(J):
                            part = group % 2 if which == 0 else group // 2
                            sp.dma_start(stack[D * group:D * (group + 1), kp % 2, which, j, :].bitcast(F32),
                                         parts[D * j:D * (j + 1), 2 * which + part, :].bitcast(F32)
                                         ).then_inc(stacked[kp % 2][which][j], 16)

            run_steps(sp, step)

        @block.tensor
        def _(pe):
            def rows(n, kn, o):
                if o % T == 0:
                    for which in range(2):
                        pe.wait_ge(stacked[(kn // 2) % 2][which][o // T],
                                   nth(half(n, kn, -(kn % 2)), kn // 2) * (J * 16) + J * 16)
                wait(pe, rows_used, 8 * n + o - 1)
                if isinstance(n, int) and n == 0 and o == 0:
                    pe.wait_ge(kq_high, 4)
                q, key = head(kn // 2, 1, o, kn % 2), head(kn // 2, 0, o, kn % 2)
                for t in range(T):
                    last = nc.tensor.matmul(row_bank[o % 2][:, t * S:(t + 1) * S], q[:, t * P:(t + 1) * P], key,
                                            start=(t == 0), stop=True, skip_group_check=True)
                last.then_inc(rows_made, 1)

            def cols(g, k, o):
                if isinstance(g, int) and g == 0 and o == 0:
                    pe.wait_ge(kq_high, 8)
                this_use = bank_slot(k, o)
                last_use = max(n for n in range(this_use - BODY * H, this_use)
                               if n % (BODY * H) % COLUMN_BANKS == this_use % COLUMN_BANKS)
                wait(pe, probs_ready, 8 * g + o - (this_use - last_use) + 1)
                q, key = head(k // 2, 1, o, k % 2), head(k // 2, 0, o, k % 2)
                for t in range(T):
                    last = nc.tensor.matmul(col(k, o)[:, t * S:(t + 1) * S],
                                            key[:, t * P:(t + 1) * P], q,
                                            start=(t == 0), stop=True, skip_group_check=True)
                last.then_inc(cols_made, 1)

            def subtract_top(g, k, o):
                if o == 0:
                    pe.wait_ge(shift_ready, g + 1)
                    if isinstance(g, int) and g == 0:
                        pe.wait_ge(picked, 1)
                pe.wait_ge(masked, 8 * g + o + 1)
                nc.tensor.matmul(col(k, o)[:], pick[:, o, :],
                                 shift[:, k % 2].unsqueeze(1).to_broadcast([ROWS, T, S]),
                                 start=False, stop=True, skip_group_check=True).then_inc(shifted, 1)

            def turn_top(g, k):
                pe.wait_ge(top_cut, g + 1)
                pe.wait_ge(v_ready, min(g + 2, B) if isinstance(g, int) else g + 2)
                wait(pe, y_ready, g - 2)
                for t in range(T):
                    last = nc.tensor.transpose(out_bank[0:ROWS, t * P:(t + 1) * P],
                                               cut_top[:, k % 2, t, :].bitcast(F32), ident[:])
                last.then_inc(top_turned, 1)

            def project_kq(pair, kp, c, half_):
                if c == 0:
                    pe.wait_ge((xt_high, xt_low)[half_], 2 * pair + 2)
                if half_ == 0:
                    if isinstance(pair, int) and pair == 0 and c in (0, 2):
                        pe.wait_ge(w_cut, c // 2 + 1)
                    if not isinstance(pair, int) or pair > 1:
                        wait(pe, kq_high, 4 * pair + c)
                    elif pair == 1:
                        pe.wait_ge(kq_high, 4)
                features = slice((c % 2) * P, (c % 2 + 1) * P)
                terms = len(TERMS) // 2
                for n, (b, a, t) in enumerate(TERMS[half_ * terms:(half_ + 1) * terms]):
                    last = nc.tensor.matmul(kq_bank(pair, c)[:], w_parts[:, a, c // 2, t, features],
                                            xt_parts[:, kp % 2, b, t, :], start=(half_ == 0 and n == 0),
                                            stop=(half_ == 1 and n == terms - 1), skip_group_check=True)
                if half_ == 1:
                    last.then_inc(kq_made, 1)

            def project_v(n, kn):
                if isinstance(n, int) and n == 0:
                    pe.wait_ge(w_cut, 4)
                    pe.wait_ge(bias_ready, 1)
                wait(pe, shift_ready, n - 1)
                wait(pe, y_ready, n - 4)
                wait(pe, v_ready, n)
                for tile in range(T):
                    nodes = slice((kn % 2) * S + tile * P, (kn % 2) * S + (tile + 1) * P)
                    for i, (a, c, t) in enumerate(TERMS):
                        last = nc.tensor.matmul(out_bank[:, tile * E:(tile + 1) * E],
                                                xt_parts[:, (kn // 2) % 2, a, t, nodes],
                                                w_parts[:, c, 2, t, :], start=(tile == 0 and i == 0),
                                                stop=(i == len(TERMS) - 1), skip_group_check=True)
                last.then_inc(v_made, 1)

            def weigh_v(g, k, half_):
                if half_ == 0:
                    pe.wait_ge(v_ready, g + 1)
                if context_bank(g, half_) is row_bank[0]:
                    pe.wait_ge(rows_used, 8 * B)
                else:
                    wait(pe, ctx_ready, 2 * g + half_)
                pe.wait_ge(probs_ready, 8 * g + J * half_ + J)
                for t in range(T):
                    for o in range(J * half_, J * half_ + J):
                        c = D * (o % J)
                        nc.tensor.matmul(context_bank(g, half_)[c:c + D, 0:S],
                                         v[:, (k // 2) % 2, k % 2, t, o * D:(o + 1) * D],
                                         probs[:, o, t * S:(t + 1) * S], start=(t == 0), stop=(t == T - 1),
                                         tile_position=(0, c))

            def sum_probs(g, half_):
                pe.wait_ge(folded_ready, 4 * g + 2 * half_ + 2)
                for o in range(J * half_, J * half_ + J):
                    c = D * (o % J)
                    last = nc.tensor.matmul(context_bank(g, half_)[c:c + D, S:2 * S], ones[:, 0:D], folded[:, o, :],
                                            start=True, stop=True, tile_position=(0, c))
                last.then_inc(ctx_made, 1)

            def project_out(g, k, n):
                if n == 0:
                    pe.wait_ge(ctx_low, 2 * g + 2)
                    pe.wait_ge(v_ready, min(g + 5, B) if isinstance(g, int) else g + 5)
                    pe.wait_ge(shift_ready, min(g + 3, B) if isinstance(g, int) else g + 3)
                    wait(pe, y_ready, g)
                nodes = slice(n * P, (n + 1) * P)
                for i, (a, b, f) in enumerate(TERMS):
                    last = nc.tensor.matmul(out_bank[:, n * E:(n + 1) * E], ctx_parts[:, k % 2, a, f, nodes],
                                            w_parts[:, b, 3, f, :], start=(n == 0 and i == 0),
                                            stop=(i == len(TERMS) - 1), skip_group_check=True)
                if n == T - 1:
                    last.then_inc(out_made, 1)

            def make_bias():
                pe.wait_ge(constants, 1)
                pe.wait_ge(biases_in, 4 * 16)
                pe.wait_ge(weight_in[3], 16)
                nc.tensor.matmul(out_bank[:, 0:E], ones[0:1, :], b_o[:], start=True, stop=False)
                for f in range(T):
                    last = nc.tensor.matmul(out_bank[:, 0:E], b_v[:, f:f + 1].to_broadcast([P, P]),
                                            w_whole[:, 3, f, :], start=False, stop=(f == T - 1))
                last.then_inc(bias_made, 1)

            def step(g, k):
                do = todo(g, k)
                if isinstance(g, int) and g == -2:
                    make_bias()
                for o in range(H):
                    if do["cols"]:
                        cols(g, k, o)
                    if o == 0 and do["before"]:
                        subtract_top(g - 1, k - 1, H - 1)
                    if o > 0 and do["cols"]:
                        subtract_top(g, k, o - 1)
                    if do["rows"] and o < H - 1:
                        rows(g + 1, k + 1, o + 1)
                    if do["next rows"] and o == H - 1:
                        rows(g + 2, k + 2, 0)
                    if o == 2 and do["before"]:
                        weigh_v(g - 1, k - 1, 1)
                    if o == 3 and do["before"]:
                        sum_probs(g - 1, 1)
                    if o == 1 and do["v"]:
                        project_v(g + 2, k + 2)
                    if (k % 2, o) in OUT_SLOTS and do["second"]:
                        project_out(g - 2, k - 2, OUT_SLOTS[k % 2, o])
                    if o == 6 and do["cols"]:
                        weigh_v(g, k, 0)
                    if do["kq"] and (k % 2, o) in KQ_SLOTS:
                        project_kq(half(g, k, 3 + (k + 1) % 2), (k + 4) // 2, *KQ_SLOTS[k % 2, o])
                    if o == 7 and do["cols"]:
                        sum_probs(g, 0)
                    if o == 7 and do["rows"]:
                        turn_top(g + 1, k + 1)

            run_steps(pe, step)

        @block.vector
        def _(dve):
            def reduce_rows(n, kn, o):
                if o == 0:
                    dve.wait_ge(adj_in[(kn // 2) % 2], nth(half(n, kn, -(kn % 2)), kn // 2) * 16 + 16)
                dve.wait_ge(rows_made, 8 * n + o + 1)
                stand_apart(dve, passed_dve)
                for t in range(T):
                    tile = row_bank[o % 2][:, t * S:(t + 1) * S]
                    last = nc.vector.tensor_tensor_reduce(
                        tile, tile, adj_rows[:, (kn // 2) % 2, kn % 2, t, :], 1.0, LOWEST, ALU.mult, ALU.max,
                        top[:, kn % 2, t, o:o + 1])
                last.then_inc(rows_used, 1)

            def cut_tops(n, kn):
                dve.wait_ge(rows_used, 8 * n + 8)
                high, low = cut_top[:, kn % 2, :, 0:H], cut_top[:, kn % 2, :, LOW:ROWS]
                nc.vector.tensor_scalar(high, top[:, kn % 2], -1.0, None, ALU.mult).then_inc(top_high, 1)
                dve.wait_ge(top_high, n + 1)
                nc.vector.scalar_tensor_tensor(low, top[:, kn % 2], -1.0, high.bitcast(F32),
                                               ALU.mult, ALU.subtract).then_inc(top_cut, 1)

            def mask_cols(g, k, o):
                if o == 0:
                    dve.wait_ge(adj_t_in[(k // 2) % 2], nth(half(g, k, -(k % 2)), k // 2) * 16 + 16)
                dve.wait_ge(cols_made, 8 * g + o + 1)
                tile = col(k, o)[:]
                nc.vector.tensor_tensor(tile, tile, adj_cols[:, (k // 2) % 2, k % 2].rearrange("p t s -> p (t s)"),
                                        ALU.mult).then_inc(masked, 1)

            def scale_context(g, half_):
                dve.wait_ge(inverted, 2 * g + half_ + 1)
                wait(dve, ctx_low, 2 * g + half_ - 1)
                nc.vector.tensor_tensor(context[:, half_, :], context_bank(g, half_)[:, 0:S], inverse[:],
                                        ALU.mult).then_inc(ctx_ready, 1)

            def add_residual(g, k):
                dve.wait_ge(out_made, g + 1)
                dve.wait_ge(x_ready, g + 1)
                wait(dve, result_ready, g)
                nc.vector.tensor_tensor(y[:].rearrange("p t e -> p (t e)"), out_bank[:],
                                        xr[:, (k // 2) % 2, k % 2].rearrange("p t e -> p (t e)"),
                                        ALU.add).then_inc(y_ready, 1)

            def row_stats(g, t):
                dve.wait_ge(y_ready, g + 1)
                nc.vector.bn_stats(stats[:, t, :], y[:, t, :]).then_inc(stats_ready, 1)

            def aggregate(g):
                dve.wait_ge(stats_ready, T * (g + 1))
                stand_apart(dve, passed_dve)
                for t in range(T):
                    last = nc.vector.bn_aggr(mean_var[:, t, :], stats[:, t, :])
                last.then_inc(mean_ready, 1)

            nc.vector.memset(cut_top[:].bitcast(F32), 0.0)
            nc.vector.memset(scale[:, 1, :], -0.5)
            nc.vector.memset(ones[:], 1.0).then_inc(cleared, 1)
            for n in range(4):
                high = w_parts[:, 0, n].rearrange("p t e -> p (t e)")
                tile = w_whole[:, n].rearrange("p t e -> p (t e)")
                dve.wait_ge(weight_in[n], 16)
                nc.vector.tensor_copy(high, tile).then_inc(w_high, 1)
                dve.wait_ge(w_high, n + 1)
                nc.vector.tensor_tensor(w_parts[:, 1, n].rearrange("p t e -> p (t e)"), tile, high.bitcast(F32),
                                        ALU.subtract).then_inc(w_cut, 1)
            dve.wait_ge(drafted, 3)
            nc.vector.tensor_copy(pick[:], draft).then_inc(picked, 1)
            dve.wait_ge(bias_made, 1)
            nc.vector.tensor_copy(bias[:], out_bank[:, 0:E]).then_inc(bias_ready, 1)
            for which, j in ((0, 3), (1, 0), (1, 2)):
                stack_first(dve, nc.vector.tensor_copy, which, j)

            def step(g, k):
                do = todo(g, k)
                for o in range(H):
                    if do["cols"]:
                        mask_cols(g, k, o)
                    if do["rows"] and o < H - 1:
                        reduce_rows(g + 1, k + 1, o + 1)
                    if do["next rows"] and o == H - 1:
                        reduce_rows(g + 2, k + 2, 0)
                    if do["rows"] and o == H - 2:
                        cut_tops(g + 1, k + 1)
                    if do["before"] and o == 1:
                        scale_context(g - 1, 0)
                    if do["before"] and o == 5:
                        scale_context(g - 1, 1)
                    if do["third"] and o == 0:
                        row_stats(g - 3, 0)
                    if do["third"] and o == 1:
                        row_stats(g - 3, 1)
                    if do["second"] and o == 6:
                        add_residual(g - 2, k - 2)
                    if do["third"] and o == 2:
                        aggregate(g - 3)

            run_steps(dve, step)

        @block.scalar
        def _(act):
            def load_masks(pair, kp):
                wait(act, masked, 16 * (pair - 1))
                act.dma_start(flat(adj_rows[:, kp % 2]), adj[pair]).then_inc(adj_in[kp % 2], 16)
                act.dma_start(flat(adj_cols[:, kp % 2]), adj_t[pair]).then_inc(adj_t_in[kp % 2], 16)

            def load_x(pair, kp):
                wait(act, y_ready, 2 * (pair - 1))
                act.dma_start(flat(xr[:, kp % 2]), x[pair]).then_inc(x_in[kp % 2], 16)

            def exp(g, k, o):
                act.wait_ge(shifted, 8 * g + o + 1)
                if isinstance(g, int) and g == 0 and o == 0:
                    act.wait_ge(bias_ready, 1)
                if o % J == 0:
                    wait(act, ctx_made, 2 * g - 1 + o // J)
                nc.scalar.activation(probs[:, o, :], col(k, o)[:], ACT.Exp,
                                     scale=2.0 * float(D) ** -0.5).then_inc(probs_ready, 1)

            def invert(g, half_):
                act.wait_ge(ctx_made, 2 * g + half_ + 1)
                wait(act, ctx_ready, 2 * g + half_)
                nc.scalar.activation(inverse[:], context_bank(g, half_)[:, S:2 * S], ACT.Ln).then_inc(logs_ready, 1)
                act.wait_ge(logs_ready, 2 * g + half_ + 1)
                nc.scalar.activation(inverse[:], inverse[:], ACT.Exp, scale=-1.0).then_inc(inverted, 1)

            def cut_context(g, k, half_):
                act.wait_ge(ctx_ready, 2 * g + half_ + 1)
                wait(act, out_made, g - 1)
                nc.scalar.copy(ctx_parts[:, k % 2, 0, half_, :], context[:, half_, :]).then_inc(ctx_high, 1)

            def cut_x(pair, kp, t):
                if t == 0:
                    act.wait_ge(xt_in, 16 * pair + 16)
                    wait(act, v_made, 2 * pair - 2)
                nc.scalar.copy(xt_parts[:, kp % 2, 0, t, :], xt[:, t, :]).then_inc(xt_high, 1)

            def copy_shift(g, k):
                act.wait_ge(top_turned, g + 1)
                nc.scalar.copy(shift[:, k % 2], out_bank[0:ROWS, 0:S]).then_inc(shift_ready, 1)

            def cut_kq(pair, kp, c):
                act.wait_ge(kq_made, 4 * pair + c + 1)
                wait(act, kq_low, 4 * pair + c - 1)
                if c % 2 == 0:
                    last = pair - 1
                    for j in range(J):
                        wait(act, stacked[(kp - 1) % 2][c // 2][j], nth(last, kp - 1) * (J * 16) + J * 16
                             if not isinstance(pair, int) or pair > 0 else 0)
                if isinstance(pair, int) and pair == 0 and c == 0:
                    act.wait_ge(biases_in, 4 * 16)
                b = (b_k if c < 2 else b_q)[:, c % 2:c % 2 + 1]
                nc.scalar.activation(whole[:, c % 2, :], kq_bank(pair, c)[:], ACT.Identity, bias=b)
                nc.scalar.activation(parts[:, 2 * (c // 2), (c % 2) * 512:(c % 2 + 1) * 512],
                                     kq_bank(pair, c)[:], ACT.Identity, bias=b).then_inc(kq_high, 1)

            def copy_v(n, kn):
                act.wait_ge(v_made, n + 1)
                nc.scalar.copy(v[:, (kn // 2) % 2, kn % 2].rearrange("p t e -> p (t e)"),
                               out_bank[:]).then_inc(v_ready, 1)

            def normalise(g, k):
                act.wait_ge(scale_ready, g + 1)
                act.wait_ge(stored[k % 2], half(g, k, -(k % 2)) * 16 + 16)
                for t in range(T):
                    last = nc.scalar.activation(result[:, k % 2, t, :], y[:, t, :], ACT.Identity,
                                                bias=scale[:, 3, t:t + 1], scale=scale[:, 2, t:t + 1])
                last.then_inc(result_ready, 1)

            def store(g, k):
                act.wait_ge(result_ready, g + 1)
                act.dma_start(out_d[g], result[:, k % 2]).then_inc(stored[k % 2], 16)

            for n in range(2):
                act.sem_inc(stored[n], 16)
            nc.scalar.preload_act_table_set("natural_log_exp_and_others")

            def step(g, k):
                do = todo(g, k)
                for o in range(H):
                    if isinstance(g, int) and g == -2 and o == 3:
                        stack_first(act, nc.scalar.copy, 1, 1)
                        stack_first(act, nc.scalar.copy, 1, 3)
                    if o == 0 and do["cols"]:
                        copy_shift(g, k)
                    if o == 1 and k % 2 == 0 and do["v"]:
                        load_masks(half(g, k, 2), (k + 2) // 2)
                    if o == 2 and k % 2 == 0 and do["cols"]:
                        load_x(half(g, k, 0), k // 2)
                    if o == 0 and do["before"]:
                        exp(g - 1, k - 1, H - 1)
                    if o > 0 and do["cols"]:
                        exp(g, k, o - 1)
                    if do["kq"] and (k % 2, o) in KQ_CUT_SLOTS:
                        cut_kq(half(g, k, 3 + (k + 1) % 2), (k + 4) // 2, KQ_CUT_SLOTS[k % 2, o])
                    if do["v"] and o == 3:
                        copy_v(g + 2, k + 2)
                    if do["before"] and o == 0:
                        invert(g - 1, 0)
                    if do["before"] and o == 4:
                        invert(g - 1, 1)
                    if do["before"] and o == 2:
                        cut_context(g - 1, k - 1, 0)
                    if do["before"] and o == 6:
                        cut_context(g - 1, k - 1, 1)
                    if do["x"] and (k % 2, o) in X_SLOTS:
                        cut_x(half(g, k, 4), (k + 4) // 2, X_SLOTS[k % 2, o])
                    if do["third"] and o == 6:
                        store(g - 3, k - 3)
                    if do["third"] and o == 4:
                        normalise(g - 3, k - 3)

            run_steps(act, step)
            for n in range(2):
                act.wait_ge(stored[n], 16 * (B // 2) + 16)

        @block.gpsimd
        def _(pool):
            def low_kq(pair, kp, c):
                pool.wait_ge(kq_high, 4 * pair + c + 1)
                cut = slice((c % 2) * 512, (c % 2 + 1) * 512)
                nc.gpsimd.tensor_tensor(parts[:, 2 * (c // 2) + 1, cut], whole[:, c % 2, :],
                                        parts[:, 2 * (c // 2), cut].bitcast(F32),
                                        ALU.subtract).then_inc(kq_low, 1)

            def low_x(pair, kp, t):
                pool.wait_ge(xt_high, 2 * pair + t + 1)
                nc.gpsimd.tensor_tensor(xt_parts[:, kp % 2, 1, t, :], xt[:, t, :],
                                        xt_parts[:, kp % 2, 0, t, :].bitcast(F32),
                                        ALU.subtract).then_inc(xt_low, 1)

            def low_context(g, k, half_):
                pool.wait_ge(ctx_high, 2 * g + half_ + 1)
                nc.gpsimd.tensor_tensor(ctx_parts[:, k % 2, 1, half_, :], context[:, half_, :],
                                        ctx_parts[:, k % 2, 0, half_, :].bitcast(F32), ALU.subtract).then_inc(ctx_low, 1)

            def fold(g, i):
                pool.wait_ge(probs_ready, 8 * g + 2 * i + 2)
                wait(pool, ctx_made, 2 * g - 1 + i // 2)
                nc.gpsimd.tensor_tensor(folded[:, 2 * i:2 * i + 2, :], probs[:, 2 * i:2 * i + 2, 0:S],
                                        probs[:, 2 * i:2 * i + 2, S:2 * S], ALU.add).then_inc(folded_ready, 1)

            def add_bias(pair, kp, b):
                if b == 0:
                    if isinstance(pair, int) and pair == 0:
                        pool.wait_ge(bias_ready, 1)
                    pool.wait_ge(x_in[kp % 2], nth(pair, kp) * 16 + 16)
                tile = xr[:, kp % 2, b]
                nc.gpsimd.tensor_tensor(tile, tile, bias[:].unsqueeze(1).to_broadcast([P, T, E]),
                                        ALU.add).then_inc(x_ready, 1)

            def make_scale(g):
                pool.wait_ge(mean_ready, g + 1)
                stand_apart(pool, passed_pool)
                nc.gpsimd.tensor_scalar(scale[:, 0, :], mean_var[:, :, 1], EPS, 1.0, ALU.add,
                                        ALU.mult).then_inc(var_added, 1)
                pool.wait_ge(var_added, g + 1)
                nc.gpsimd.tensor_tensor(scale[:, 2, :], scale[:, 0, :], scale[:, 1, :],
                                        ALU.pow).then_inc(sd_inverted, 1)
                pool.wait_ge(sd_inverted, 2 * g + 1)
                nc.gpsimd.tensor_tensor(scale[:, 3, :], mean_var[:, :, 0], scale[:, 2, :],
                                        ALU.mult).then_inc(sd_inverted, 1)
                pool.wait_ge(sd_inverted, 2 * g + 2)
                stand_apart(pool, passed_pool)
                nc.gpsimd.tensor_scalar(scale[:, 3, :], scale[:, 3, :], -1.0, 0.0, ALU.mult,
                                        ALU.add).then_inc(scale_ready, 1)

            nc.gpsimd.memset(ident[:], 0.0)
            nc.gpsimd.memset(draft, 0.0).then_inc(drafted, 1)
            pool.wait_ge(drafted, 1)
            nc.gpsimd.affine_select(out=ident[:], in_=ident[:], compare_op=ALU.not_equal, fill=1.0, base=0,
                                    pattern=[[-1, P]], channel_multiplier=1)
            nc.gpsimd.affine_select(out=draft, in_=draft, compare_op=ALU.not_equal, fill=1.0, base=0,
                                    pattern=[[-1, H], [0, P]], channel_multiplier=1).then_inc(drafted, 1)
            pool.wait_ge(drafted, 2)
            nc.gpsimd.affine_select(out=draft, in_=draft, compare_op=ALU.not_equal, fill=1.0, base=-LOW,
                                    pattern=[[-1, H], [0, P]], channel_multiplier=1).then_inc(drafted, 1)
            pool.wait_ge(cleared, 1)
            pool.wait_ge(drafted, 3)
            pool.memset(folded[:, 0, 0:1], 0.0).then_inc(constants, 1)

            def step(g, k):
                do = todo(g, k)
                for o in range(H):
                    if do["before"] and o == 1:
                        fold(g - 1, 3)
                    if do["cols"] and o in {3: 0, 5: 1, 6: 2}:
                        fold(g, {3: 0, 5: 1, 6: 2}[o])
                    if do["x"] and (k % 2, o) in X_SLOTS:
                        low_x(half(g, k, 4), (k + 4) // 2, X_SLOTS[k % 2, o])
                    if do["before"] and o == 4:
                        low_context(g - 1, k - 1, 0)
                    if do["before"] and o == 6:
                        low_context(g - 1, k - 1, 1)
                    if do["kq"] and (k % 2, o) in KQ_CUT_SLOTS:
                        low_kq(half(g, k, 3 + (k + 1) % 2), (k + 4) // 2, KQ_CUT_SLOTS[k % 2, o])
                    if do["third"] and o == 2:
                        make_scale(g - 3)
                    if do["cols"] and o == 5:
                        add_bias(half(g, k, -(k % 2)), k // 2, k % 2)

            run_steps(pool, step)


def kernel(x, adj, L0_gnn_Wq, L0_gnn_bq, L0_gnn_Wk, L0_gnn_bk, L0_gnn_Wv, L0_gnn_bv, L0_gnn_Wo, L0_gnn_bo):
    import numpy as np
    import concourse.bacc as bacc
    from concourse.bass_utils import run_bass_kernel_spmd

    def rows_in(w):
        return np.ascontiguousarray(w.transpose().reshape(T, P, -1).transpose(1, 0, 2))

    def by_tile(w):
        return w.reshape(J, T, D, -1).transpose(1, 0, 2, 3).reshape(w.shape)

    def pairs(a, order):
        a = a.reshape(PAIRS, 2, T, P, -1).transpose((0, 3, 1, 2, 4) if order == "b t" else (0, 3, 2, 1, 4))
        return np.ascontiguousarray(a.reshape(PAIRS, P, -1))

    x, adj = np.asarray(x), np.asarray(adj)
    wq, wk, wv, wo = (np.asarray(w) for w in (L0_gnn_Wq, L0_gnn_Wk, L0_gnn_Wv, L0_gnn_Wo))
    bq, bk, bv, bo = (np.asarray(b) for b in (L0_gnn_bq, L0_gnn_bk, L0_gnn_bv, L0_gnn_bo))
    data = {
        "x": pairs(x, "b t"),
        "x_t": pairs(x.transpose(0, 2, 1), "t b"),
        "adj": pairs(adj, "b t"),
        "adj_t": pairs(adj.transpose(0, 2, 1), "b t"),
        "wq": rows_in(by_tile(wq)),
        "wk": rows_in(by_tile(wk)),
        "wv": rows_in(wv),
        "wo": rows_in(wo),
        "bq": np.ascontiguousarray(by_tile(bq).reshape(T, P).transpose()),
        "bk": np.ascontiguousarray(by_tile(bk).reshape(T, P).transpose()),
        "bv": np.ascontiguousarray(bv.reshape(T, P).transpose()),
        "bo": bo.reshape(1, E),
    }
    nc = bacc.Bacc("TRN2", target_bir_lowering=False, num_devices=1)
    args = [nc.dram_tensor(f"in_{n}", a.shape, F32, kind="ExternalInput").ap() for n, a in data.items()]
    out = nc.dram_tensor("out", (B, S, E), F32, kind="ExternalOutput").ap()
    build(nc, *args, out)
    r = run_bass_kernel_spmd(nc, [{f"in_{n}": a for n, a in data.items()}], core_ids=[0])
    return r.results[0]["out"]
```
